# Optimizing a Trainium2 kernel written in Bass

```python
import numpy as np
import jax
import jax.numpy as jnp

def _softmax(x, axis=-1):
    return jax.nn.softmax(x, axis=axis)

def _gelu(x):
    return jax.nn.gelu(x, approximate=True)

def _silu(x):
    return jax.nn.silu(x)

def _sigmoid(x):
    return jax.nn.sigmoid(x)

def _layernorm(x, axis=-1, eps=1e-05):
    m = jnp.mean(x, axis=axis, keepdims=True)
    v = jnp.var(x, axis=axis, keepdims=True)
    return (x - m) / jnp.sqrt(v + eps)

def _scatter_add(tgt, idx, src, axis=0):
    return tgt.at[idx].add(src)

def _segment_sum(src, seg, n):
    return jax.ops.segment_sum(src, seg, n)
kernel_name = 'mk_gnn_preln_d1_gnn_r8_282afd'

def setup_inputs(seed: int=0):
    np.random.seed(seed)
    _w = jnp.asarray

    def _rec_inputs():
        import jax
        import jax.numpy as jnp
        _gk = jax.random.key(seed)
        x = -0.000202 + 1 * jax.random.normal(jax.random.fold_in(_gk, 1), (6250, 128), jnp.float32)
        _s = jax.random.randint(jax.random.fold_in(_gk, 2), (50000,), 0, 6250, jnp.int32)
        _d = jax.random.randint(jax.random.fold_in(_gk, 3), (50000,), 0, 6250, jnp.int32)
        _loop = jnp.arange(6250, dtype=jnp.int32)
        src = jnp.concatenate([_s, _d, _loop])
        dst = jnp.concatenate([_d, _s, _loop])
        _o = jnp.argsort(dst, stable=True)
        src = src[_o]
        dst = dst[_o]
        edge_attr_128 = -5.16925e-05 + 1.00005 * jax.random.normal(jax.random.fold_in(_gk, 11), (106250, 128), jnp.float32)
        return (x, src, dst, edge_attr_128)
    x, src, dst, edge_attr_128 = _rec_inputs()

    def _L0_gnn_setup():
        import jax, jax.numpy as jnp
        import numpy as np
        N, E, H = (6250, 100000, 128)
        EPS = 1e-07
        BN_EPS = 1e-05
        LN_EPS = 1e-05
        key = jax.random.key(seed)
        ks = jax.random.split(key, 12)
        return dict(h=jax.random.normal(ks[0], (N, H), jnp.float32), edge_index=jax.random.randint(ks[1], (2, E), 0, N, dtype=jnp.int32), edge_attr=jax.random.normal(ks[2], (E, H), jnp.float32), bn_weight=1.0 + 0.1 * jax.random.normal(ks[3], (H,), jnp.float32), bn_bias=0.1 * jax.random.normal(ks[4], (H,), jnp.float32), bn_mean=0.1 * jax.random.normal(ks[5], (H,), jnp.float32), bn_var=jax.random.uniform(ks[6], (H,), jnp.float32, 0.5, 1.5), t=jnp.array(1.0, jnp.float32), W1=jax.random.normal(ks[7], (H, 2 * H), jnp.float32) / np.float32(np.sqrt(H)), b1=jnp.zeros((2 * H,), jnp.float32), ln_weight=jnp.ones((2 * H,), jnp.float32), ln_bias=jnp.zeros((2 * H,), jnp.float32), W2=jax.random.normal(ks[8], (2 * H, H), jnp.float32) / np.float32(np.sqrt(2 * H)), b2=jnp.zeros((H,), jnp.float32))
    _L0_gnn_all = _L0_gnn_setup()
    _L0_gnn_in = {k: v for k, v in _L0_gnn_all.items() if k in ('bn_weight', 'bn_bias', 'bn_mean', 'bn_var', 't', 'W1', 'b1', 'ln_weight', 'ln_bias', 'W2', 'b2')}
    del _L0_gnn_all
    return {'x': x, 'src': src, 'dst': dst, 'edge_attr_128': edge_attr_128, 'L0_gnn_bn_weight': _L0_gnn_in['bn_weight'], 'L0_gnn_bn_bias': _L0_gnn_in['bn_bias'], 'L0_gnn_bn_mean': _L0_gnn_in['bn_mean'], 'L0_gnn_bn_var': _L0_gnn_in['bn_var'], 'L0_gnn_t': _L0_gnn_in['t'], 'L0_gnn_W1': _L0_gnn_in['W1'], 'L0_gnn_b1': _L0_gnn_in['b1'], 'L0_gnn_ln_weight': _L0_gnn_in['ln_weight'], 'L0_gnn_ln_bias': _L0_gnn_in['ln_bias'], 'L0_gnn_W2': _L0_gnn_in['W2'], 'L0_gnn_b2': _L0_gnn_in['b2']}

def reference(x, src, dst, edge_attr_128, L0_gnn_bn_weight, L0_gnn_bn_bias, L0_gnn_bn_mean, L0_gnn_bn_var, L0_gnn_t, L0_gnn_W1, L0_gnn_b1, L0_gnn_ln_weight, L0_gnn_ln_bias, L0_gnn_W2, L0_gnn_b2):
    import jax
    import jax.numpy as jnp

    def _L0_gnn_ref(h, edge_index, edge_attr, bn_weight, bn_bias, bn_mean, bn_var, t, W1, b1, ln_weight, ln_bias, W2, b2):
        import jax, jax.numpy as jnp
        import numpy as np
        N, E, H = (6250, 100000, 128)
        EPS = 1e-07
        BN_EPS = 1e-05
        LN_EPS = 1e-05
        x = h
        hn = (x - bn_mean) * jax.lax.rsqrt(bn_var + BN_EPS) * bn_weight + bn_bias
        hn = jax.nn.relu(hn)
        src, dst = (edge_index[0], edge_index[1])
        msg = jax.nn.relu(hn[src] + edge_attr) + EPS
        logits = msg * t
        seg_max = jax.ops.segment_max(jax.lax.stop_gradient(logits), dst, num_segments=N)
        seg_max = jnp.where(jnp.isfinite(seg_max), seg_max, 0.0)
        ex = jnp.exp(logits - seg_max[dst])
        denom = jax.ops.segment_sum(ex, dst, num_segments=N)
        alpha = ex / (denom[dst] + 1e-16)
        agg = jax.ops.segment_sum(msg * alpha, dst, num_segments=N)
        out = agg + hn
        y = out @ W1 + b1
        mu = y.mean(-1, keepdims=True)
        var = ((y - mu) ** 2).mean(-1, keepdims=True)
        y = (y - mu) * jax.lax.rsqrt(var + LN_EPS) * ln_weight + ln_bias
        y = jax.nn.relu(y)
        y = y @ W2 + b2
        return x + y
    edge_index = jnp.stack([src, dst])
    h = jnp.maximum(_layernorm(x, axis=-1), 0.0)
    x = x + _L0_gnn_ref(h, edge_index, edge_attr_128, L0_gnn_bn_weight, L0_gnn_bn_bias, L0_gnn_bn_mean, L0_gnn_bn_var, L0_gnn_t, L0_gnn_W1, L0_gnn_b1, L0_gnn_ln_weight, L0_gnn_ln_bias, L0_gnn_W2, L0_gnn_b2)
    return x

_drawn_inputs = setup_inputs


def setup_inputs(seed=0):
    import zlib

    import numpy as np

    out = dict(_drawn_inputs(seed))
    spreads = {'L0_gnn_b1': (0.0, 0.385),
     'L0_gnn_ln_weight': (1.0, 0.2),
     'L0_gnn_ln_bias': (0.0, 0.1),
     'L0_gnn_b2': (0.0, 0.1)}
    factors = {}
    for name, (base, spread) in spreads.items():
        noise = np.random.default_rng([zlib.crc32(name.encode()), seed]).standard_normal(out[name].shape)
        drawn = base * np.exp(spread * noise) if base else spread * noise
        out[name] = jnp.asarray(drawn.astype(out[name].dtype))
    for name, factor in factors.items():
        out[name] = (out[name] * factor).astype(out[name].dtype)
    return out
```

```python
import concourse.bass as bass
from concourse import mybir
from contextlib import ExitStack

FP32 = mybir.dt.float32
BF16 = mybir.dt.bfloat16
I32 = mybir.dt.int32
ALU = mybir.AluOpType
ACT = mybir.ActivationFunctionType
AX = mybir.AxisListType

P = 128
N = 6250
E = 106250
H = 128
H2 = 2 * H
T = 13
CE = T * P
K = -(-E // CE)
EP = K * CE
SLOTS = 4
NB = 8
RB = EP // P // NB
NW = 6250 + P
BIG = 1.5e38
SMEPS = 1e-7
BNEPS = 1e-5
LNEPS = 1e-5


def build(nc, x, src, dst, ea, bn_w, bn_b, bn_m, bn_v, t_in, W1, b1, ln_w, ln_b, W2, b2, out):
    hn_dram = nc.dram_tensor("hn_rows", (N, H), FP32).ap()
    xh_dram = nc.dram_tensor("xh_rows", (N, H), FP32).ap()
    cap_dram = nc.dram_tensor("cap_row", (EP + 1,), BF16).ap()

    ctx = ExitStack()
    with ctx:
        def sb(name, shape, dt=FP32):
            return ctx.enter_context(nc.sbuf_tensor(name, shape, dt))

        def sem(name):
            return ctx.enter_context(nc.semaphore(name))

        ident = sb("ident", [P, P])
        iota = sb("iota", [P, P])
        ones_row = sb("ones_row", [1, P])
        ones_row16 = sb("ones_row16", [1, P], BF16)
        ones_col = sb("ones_col", [P, 1])
        bnp = sb("bnp", [P, 4, H])
        bnA = sb("bnA", [P, H])
        bnB = sb("bnB", [P, H])
        tcol = sb("tcol", [P, 1])
        w1s = sb("w1s", [P, H2])
        w2s = sb("w2s", [P, 2, H])
        b1s = sb("b1s", [1, H2])
        b2s = sb("b2s", [1, H])
        lncol = sb("lncol", [P, 2, 2])
        capw = sb("capw", [RB, NB, P], BF16)
        cap0w = sb("cap0w", [1, 1], BF16)
        srcT = sb("srcT", [P, K * T])
        dstT = sb("dstT", [P, K * T])
        dl = sb("dl", [P, K, T])
        nbf = sb("nbf", [P, K])
        nbi = sb("nbi", [1, K], I32)
        gidx = sb("gidx", [P, SLOTS, T], I32)
        S = sb("S", [P, SLOTS, T, H])
        capr = sb("capr", [1, SLOTS, CE + 1], BF16)
        cap = sb("cap", [P, 2, CE + 1], BF16)
        zT = sb("zT", [P, 2, CE])
        Mf = sb("Mf", [P, 2, CE])
        Mb = sb("Mb", [P, 2, CE])
        ex = sb("ex", [P, 2, T, H])
        OH = sb("OH", [P, 2, T, P])
        def early(t, a):
            return t[0:RB, :, :, :].rearrange("r a j c -> r (a j c)")[:, 0:a * NB * P]
        idx_i = early(ex, 3).bitcast(I32).rearrange("r (a b p) -> r a b p", a=3, b=NB)
        idx_f = early(OH, 3).rearrange("r (a b p) -> r a b p", a=3, b=NB)
        cmp_f = early(ex, 1).rearrange("r (b p) -> r b p", b=NB)
        carry = sb("carry", [P, SLOTS, 2])
        fac = sb("fac", [P, SLOTS])
        tab = sb("tab", [P, 2, NW])
        xw = sb("xw", [P, H])
        hw = sb("hw", [P, H])
        oT = sb("oT", [P, 4, P])
        st = sb("st", [P, 6])
        xst = sb("xst", [P, 13, 6])
        xmv = sb("xmv", [P, 4, 13, 2])
        xrs = sb("xrs", [P, 4, 13])
        xnm = sb("xnm", [P, 4, 13])
        mv = sb("mv", [P, 8])
        yn = sb("yn", [P, H2])
        h2 = sb("h2", [P, 2, P])
        res = sb("res", [P, H])

        def pb(name):
            return ctx.enter_context(nc.psum_tensor(name, [P, 512], FP32))
        ping = [pb("ping0"), pb("ping1")]
        MT = ctx.enter_context(nc.psum_tensor("MT", [P, 2048], FP32))
        DN = pb("DN")
        PM = pb("PM")

        s_turn_sp = sem("sync_waited")
        s_turn_gp = sem("gpsimd_waited")
        s_turn_dve = sem("vector_waited")
        s_idx = sem("idx_rows_loaded")
        s_bn = sem("bn_loaded")
        s_x = [sem(f"x_piece_loaded{q}") for q in range(4)]
        s_xvar = sem("x_variance_ready")
        s_xsd = sem("x_std_ready")
        s_xsc = sem("x_scale_ready")
        s_h = sem("h_piece_ready")
        s_xh = sem("x_plus_h_ready")
        s_xhp = [sem(f"x_plus_h_stored{q}") for q in range(4)]
        s_par = sem("mlp_params_loaded")
        s_hnw = sem("hn_rows_stored")
        s_capw = sem("cap_row_stored")
        s_const = sem("constants_ready")
        s_dve = sem("dve_steps")
        s_act = sem("act_steps")
        s_std = sem("bn_std_ready")
        s_ab = sem("bn_affine_ready")
        s_abT = sem("bn_affine_transposed")
        s_abc = sem("bn_columns_ready")
        s_aff = sem("hn_affine_done")
        s_hn = sem("hn_piece_ready")
        s_hnp = sem("hn_stored")
        s_if = sem("idx_float_ready")
        s_capc = sem("cap_rows_ready")
        s_iT = sem("idx_transposed")
        s_iTc = sem("idx_transposes_copied")
        s_nbp = sem("window_bases_broadcast")
        s_nb = sem("window_bases_ready")
        s_ea = [sem(f"edge_attr_loaded{q}") for q in range(SLOTS)]
        s_tail = sem("edge_attr_tail_loaded")
        s_capr = [sem(f"cap_loaded{q}") for q in range(SLOTS)]
        s_gi = sem("gather_idx_ready")
        s_g = [sem(f"gathered{q}") for q in range(SLOTS)]
        s_relu = sem("relu_done")
        s_unit = sem("psum_unit_ready")
        s_evac = sem("psum_unit_evacuated")
        s_fwd = sem("forward_max_done")
        s_scan = sem("scans_done")
        s_cm = sem("carry_min_done")
        s_gap = sem("carry_gap_ready")
        s_mT = sem("max_transposed")
        s_d = sem("logit_gap_ready")
        s_fac = sem("carry_factor_ready")
        s_exp = sem("exp_done")
        s_p = sem("weighted_msg_ready")
        s_sum = sem("sums_ready")
        s_mrg = sem("chunk_merged")
        s_tab0 = sem("tables_cleared")
        s_xw = sem("x_window_loaded")
        s_xT = sem("x_window_transposed")
        s_hT = sem("hn_window_ready")
        s_o = sem("mlp_input_ready")
        s_y = sem("hidden_ready")
        s_var = sem("ln_stats_ready")
        s_sd = sem("ln_std_ready")
        s_nrm = sem("ln_scale_ready")
        s_yn = sem("hidden_normalised")
        s_yT = sem("hidden_transposed")
        s_h2 = sem("hidden_activated")
        s_o2 = sem("mlp_output_ready")
        s_res = sem("result_ready")
        s_out = sem("result_stored")

        XQ, XJ = 4, 12
        XT = N - XQ * XJ * P
        tiles = [XJ, XJ, XJ, XJ + 1]
        xq = [S[:, q, 0:tiles[q], :] for q in range(XQ)]
        hbuf = (Mf[:, 0, :], Mf[:, 1, :], Mb[:, 0, :], Mb[:, 1, :])
        hq = [hbuf[q][:, 0:tiles[q] * H].rearrange("p (j c) -> p j c", c=H) for q in range(XQ)]

        def piece(rows, q):
            return rows[0:XQ * XJ * P, :].rearrange("(p q j) c -> q p j c", p=P, q=XQ)[q]

        WT = -(-N // P)

        def window(m):
            return m * P if not isinstance(m, int) or m < WT - 1 else N - P

        block = ctx.enter_context(nc.Block())

        @block.sync
        def _(sp):
            FULL = (NB - 1) * RB * P
            last_rows = (E - FULL) // P
            sp.wait_ge(s_const, 1)
            for a, (arr, o) in enumerate(((src, 0), (dst, 0), (dst, 1))):
                sp.dma_start(idx_i[:, a, 0:NB - 1, :],
                             arr[o:o + FULL].rearrange("(b r p) -> r b p", b=NB - 1, r=RB)).then_inc(s_idx, 16)
                sp.dma_start(idx_i[0:last_rows, a, NB - 1, :],
                             arr[FULL + o:FULL + o + last_rows * P].rearrange("(r p) -> r p", p=P)).then_inc(s_idx, 16)
                rest = E - FULL - last_rows * P - o
                sp.dma_start(idx_i[last_rows:last_rows + 1, a, NB - 1, 0:rest],
                             arr[E - rest:E].rearrange("(a n) -> a n", a=1)).then_inc(s_idx, 16)
            for q in range(XQ):
                sp.dma_start(xq[q][:, 0:XJ, :], piece(x, q)).then_inc(s_x[q], 16)
            sp.dma_start(xq[XQ - 1][0:XT, XJ, :], x[N - XT:N, :]).then_inc(s_x[XQ - 1], 16)
            sp.dma_start(xq[XQ - 1][XT:P, XJ, :], x[0:P - XT, :]).then_inc(s_x[XQ - 1], 16)
            for i, v in enumerate((bn_w, bn_b, bn_m, bn_v)):
                sp.dma_start(bnp[:, i, :], v.rearrange("(a n) -> a n", a=1).to_broadcast([P, H])).then_inc(s_bn, 16)
            for q in range(XQ):
                sp.wait_ge(s_xh, q + 1)
                sp.dma_start(piece(xh_dram, q), xq[q][:, 0:XJ, :]).then_inc(s_xhp[q], 16)
                if q == XQ - 1:
                    sp.dma_start(xh_dram[N - XT:N, :], xq[q][0:XT, XJ, :]).then_inc(s_xhp[q], 16)
                sp.wait_ge(s_hn, q + 1)
                sp.dma_start(piece(hn_dram, q), hq[q][:, 0:XJ, :]).then_inc(s_hnp, 16)
                if q == XQ - 1:
                    sp.dma_start(hn_dram[N - XT:N, :], hq[q][0:XT, XJ, :]).then_inc(s_hnp, 16)
            sp.wait_ge(s_capc, 1)
            for b in range(NB):
                sp.dma_start(cap_dram[1 + b * RB * P:1 + (b + 1) * RB * P].rearrange("(r p) -> r p", p=P),
                             capw[:, b, :]).then_inc(s_capw, 16)
            sp.dma_start(cap_dram[0:1].rearrange("(a n) -> a n", a=1), cap0w[:, :]).then_inc(s_capw, 16)
            with nc.allow_non_contiguous_dma(reason="small parameter columns"):
                sp.dma_start(tcol[:, :], t_in.rearrange("(a n) -> a n", a=1).to_broadcast([P, 1])).then_inc(s_par, 16)
                sp.dma_start(lncol[:, 0, :], ln_w.rearrange("(h c) -> c h", c=H)).then_inc(s_par, 16)
                sp.dma_start(lncol[:, 1, :], ln_b.rearrange("(h c) -> c h", c=H)).then_inc(s_par, 16)
            sp.dma_start(w1s[:, :], W1).then_inc(s_par, 16)
            sp.dma_start(w2s[:, :, :], W2.rearrange("(h p) n -> p h n", p=P)).then_inc(s_par, 16)
            sp.dma_start(b1s[:, :], b1.rearrange("(a n) -> a n", a=1)).then_inc(s_par, 16)
            sp.dma_start(b2s[:, :], b2.rearrange("(a n) -> a n", a=1)).then_inc(s_par, 16)
            sp.wait_ge(s_capw, 16 * (NB + 1))

            def load(k, slot, first):
                if first:
                    sp.wait_ge(s_xhp[slot], 16 if slot < XQ - 1 else 32)
                else:
                    sp.wait_ge(s_sum, k - SLOTS + 1)
                    sp.sem_inc(s_turn_sp, 1)
                if isinstance(k, int) and k == K - 1:
                    full = (E - k * CE) // P
                    rest = E - k * CE - full * P
                    sp.dma_start(S[:, slot, 0:full, :],
                                 ea[k * CE:k * CE + full * P, :].rearrange("(j p) c -> p j c", p=P)).then_inc(s_tail, 16)
                    sp.dma_start(S[0:rest, slot, full, :], ea[E - rest:E, :]).then_inc(s_tail, 16)
                    sp.dma_start(S[rest:P, slot, full, :], ea[0:P - rest, :]).then_inc(s_tail, 16)
                    for j in range(full + 1, T):
                        sp.dma_start(S[:, slot, j, :], ea[0:P, :]).then_inc(s_tail, 16)
                else:
                    sp.dma_start(S[:, slot, :, :],
                                 ea[bass.ds(k * CE, CE), :].rearrange("(j p) c -> p j c", p=P)).then_inc(s_ea[slot], 16)
                sp.dma_start(capr[0:1, slot, :],
                             cap_dram[bass.ds(k * CE, CE + 1)].rearrange("(a n) -> a n", a=1)).then_inc(s_capr[slot], 16)
            for k in range(SLOTS):
                load(k, k, True)
            with sp.Fori(1, K // SLOTS - 1) as i:
                for u in range(SLOTS):
                    load(i * SLOTS + u, u, False)
            for k in range(K - SLOTS, K):
                load(k, k % SLOTS, False)

            def mlp(m):
                wb = window(m)
                if not isinstance(m, int) or m > 0:
                    sp.wait_ge(s_res, m)
                    sp.sem_inc(s_turn_sp, 1)
                sp.dma_start(xw[:, :], xh_dram[bass.ds(wb, P), :]).then_inc(s_xw, 16)
                sp.dma_start(hw[:, :], hn_dram[bass.ds(wb, P), :]).then_inc(s_xw, 16)
                sp.wait_ge(s_res, m + 1)
                sp.sem_inc(s_turn_sp, 1)
                sp.dma_start(out[bass.ds(wb, P), :], res[:, :]).then_inc(s_out, 16)
                sp.wait_ge(s_out, (m + 1) * 16)
                sp.sem_inc(s_turn_sp, 1)
            for m in range(1):
                mlp(m)
            with sp.Fori(1, WT - 1) as m:
                mlp(m)
            mlp(WT - 1)

        @block.gpsimd
        def _(gp):
            gp.memset(idx_i[:, 0, NB - 1, :], 0)
            gp.memset(idx_i[:, 1:3, NB - 1, :], N).then_inc(s_const, 1)
            gp.memset(ident[:, :], 0.0).then_inc(s_const, 1)
            gp.wait_ge(s_const, 2)
            gp.affine_select(out=ident[:, :], in_=ident[:, :], compare_op=ALU.not_equal, fill=1.0, base=0,
                             pattern=[[-1, P]], channel_multiplier=1).then_inc(s_const, 1)
            gp.iota(iota[:, :], [[1, P]], base=0, channel_multiplier=0,
                    allow_small_or_imprecise_dtypes=True).then_inc(s_const, 1)
            gp.memset(ones_row[:, :], 1.0)
            gp.memset(ones_row16[:, :], 1.0)
            gp.memset(cap0w[:, :], -BIG)
            gp.memset(ones_col[:, :], 1.0).then_inc(s_const, 1)
            gp.memset(tab[:, :, :], 0.0).then_inc(s_tab0, 1)
            for q in range(XQ):
                gp.wait_ge(s_h, q + 1)
                gp.tensor_tensor(xq[q], xq[q], hq[q], ALU.add).then_inc(s_xh, 1)
            gp.wait_ge(s_hnp, 16 * (XQ + 1))

            def gather(k, slot):
                gp.wait_ge(s_gi, k + 1)
                if isinstance(k, int) and k == K - 1:
                    gp.wait_ge(s_tail, 16 * (3 + T - 1 - (E - k * CE) // P))
                else:
                    gp.wait_ge(s_ea[slot], (k // SLOTS + 1) * 16 if isinstance(k, int) else (k - slot) * (16 // SLOTS) + 16)
                gp.sem_inc(s_turn_gp, 1)
                for j in range(T):
                    gp.indirect_dma_start(S[:, slot, j, :], None, hn_dram[:, :],
                                          bass.IndirectOffsetOnAxis(ap=gidx[:, slot, j:j + 1], axis=0),
                                          compute_op=ALU.add).then_inc(s_g[slot], 16)
            for k in range(SLOTS):
                gather(k, k)
            with gp.Fori(1, K // SLOTS - 1) as i:
                for u in range(SLOTS):
                    gather(i * SLOTS + u, u)
            for k in range(K - SLOTS, K):
                gather(k, k % SLOTS)

        @block.scalar
        def _(act):
            act.wait_ge(s_std, 1)
            act.activation(bnp[:, 3, :], bnp[:, 3, :], ACT.Sqrt).then_inc(s_std, 1)

            def normalise(q):
                act.wait_ge(s_xvar, q + 1)
                act.activation(xrs[:, q, :], xmv[:, q, :, 1], ACT.Sqrt).then_inc(s_xsd, 1)
                act.wait_ge(s_xsc, q + 1)
                for j in range(tiles[q]):
                    ins = act.activation(hq[q][:, j, :], xq[q][:, j, :], ACT.Relu,
                                         bias=xnm[:, q, j:j + 1], scale=xrs[:, q, j:j + 1])
                ins.then_inc(s_h, 1)

            def relu_hn(q):
                act.wait_ge(s_aff, q + 1)
                act.activation(hq[q], hq[q], ACT.Relu).then_inc(s_hn, 1)
            normalise(0)
            for q in range(1, XQ):
                normalise(q)
                relu_hn(q - 1)
            relu_hn(XQ - 1)
            act.wait_ge(s_iTc, 2)
            for k in range(SLOTS):
                act.activation(gidx[:, k, :], srcT[:, k * T:(k + 1) * T], ACT.Copy).then_inc(s_gi, 1)
            act.wait_ge(s_par, 16 * 7)

            def stage1(k, slot, par, early):
                def runs(v):
                    return (v // SLOTS) if isinstance(v, int) else None
                rounds = (k // SLOTS + 1) * T * 16 if isinstance(k, int) else (k - slot) * (T * 16 // SLOTS) + T * 16
                act.wait_ge(s_g[slot], rounds)
                act.activation(S[:, slot, :, :], S[:, slot, :, :], ACT.Relu).then_inc(s_relu, 1)
                if not (isinstance(k, int) and k >= K - SLOTS):
                    act.activation(gidx[:, slot, :], srcT[:, bass.ds((k + SLOTS) * T, T)], ACT.Copy).then_inc(s_gi, 1)
                if not early:
                    act.wait_ge(s_scan, k - 1)
                    act.wait_ge(s_gap, k - 1)
                for u in range(8):
                    g = u // 2
                    n = min(512, CE + 1 - 512 * g) if u % 2 == 0 else min(512, CE - 512 * g)
                    act.wait_ge(s_unit, k * 8 + u + 1)
                    if u % 2 == 0:
                        act.activation(cap[:, par, 512 * g:512 * g + n], ping[0][:, 0:n], ACT.Copy).then_inc(s_evac, 1)
                    else:
                        act.activation(zT[:, par, 512 * g:512 * g + n], ping[1][:, 0:n], ACT.Copy,
                                       scale=tcol[:, 0:1]).then_inc(s_evac, 1)

            def stage2(k, slot, par):
                act.wait_ge(s_gap, k + 1)
                act.activation(fac[:, slot:slot + 1], carry[:, slot, 1:2], ACT.Exp).then_inc(s_fac, 1)
                act.wait_ge(s_d, k + 1)
                act.activation(ex[:, par, :, :], ex[:, par, :, :], ACT.Exp).then_inc(s_exp, 1)

            for k in range(SLOTS):
                stage1(k, k, k % 2, k < 2)
                if k:
                    stage2(k - 1, k - 1, (k - 1) % 2)
            with act.Fori(1, K // SLOTS - 1) as i:
                for u in range(SLOTS):
                    stage1(i * SLOTS + u, u, u % 2, False)
                    stage2(i * SLOTS + u - 1, (u - 1) % SLOTS, (u - 1) % 2)
            for k in range(K - SLOTS, K):
                stage1(k, k % SLOTS, k % 2, False)
                stage2(k - 1, (k - 1) % SLOTS, (k - 1) % 2)
            stage2(K - 1, (K - 1) % SLOTS, (K - 1) % 2)

            def mlp(m):
                act.wait_ge(s_var, m + 1)
                act.activation(mv[:, 3:4], mv[:, 2:3], ACT.Sqrt).then_inc(s_sd, 1)
                act.wait_ge(s_nrm, m + 1)
                act.activation(yn[:, :], PM[:, 0:H2], ACT.Identity, bias=mv[:, 5:6], scale=mv[:, 4:5]).then_inc(s_yn, 1)
                act.wait_ge(s_yT, m + 1)
                act.activation(h2[:, 0, :], PM[:, 256:384], ACT.Relu, bias=lncol[:, 1, 0:1], scale=lncol[:, 0, 0:1])
                act.activation(h2[:, 1, :], PM[:, 384:512], ACT.Relu, bias=lncol[:, 1, 1:2], scale=lncol[:, 0, 1:2]).then_inc(s_h2, 1)
            mlp(0)
            with act.Fori(1, WT - 1) as m:
                mlp(m)
            mlp(WT - 1)

        @block.vector
        def _(v):
            count = [0]

            def link(ins):
                count[0] += 1
                ins.then_inc(s_dve, 1)
                v.wait_ge(s_dve, count[0])

            v.wait_ge(s_bn, 64)
            link(v.tensor_scalar(bnp[:, 3, :], bnp[:, 3, :], BNEPS, None, ALU.add))
            v.tensor_copy(bnA[:, 0:1], bnp[:, 3, 0:1]).then_inc(s_std, 1)
            v.wait_ge(s_std, 2)
            link(v.reciprocal(bnp[:, 3, :], bnp[:, 3, :]))
            link(v.tensor_tensor(bnA[:, :], bnp[:, 3, :], bnp[:, 0, :], ALU.mult))
            link(v.tensor_tensor(bnB[:, :], bnp[:, 2, :], bnA[:, :], ALU.mult))
            v.tensor_tensor(bnB[:, :], bnp[:, 1, :], bnB[:, :], ALU.subtract).then_inc(s_ab, 1)
            v.wait_ge(s_ab, 1)
            v.wait_ge(s_idx, 16 * 9)
            v.tensor_copy(idx_f[:, :, :, :], idx_i[:, :, :, :]).then_inc(s_if, 1)
            def stats(q):
                v.wait_ge(s_x[q], 16 if q < XQ - 1 else 48)
                for j in range(tiles[q]):
                    ins = v.bn_stats(xst[:, j, :], xq[q][:, j, :])
                link(ins)
                for j in range(tiles[q]):
                    ins = v.bn_aggr(xmv[:, q, j, :], xst[:, j, :])
                link(ins)
                if tiles[q] < 13:
                    link(v.memset(xmv[:, q, 12, :], 1.0))
                v.tensor_scalar(xmv[:, q, :, 1], xmv[:, q, :, 1], LNEPS, None, ALU.add).then_inc(s_xvar, 1)
                v.wait_ge(s_xsd, q + 1)
                link(v.reciprocal(xrs[:, q, :], xrs[:, q, :]))
                v.scalar_tensor_tensor(xnm[:, q, :], xmv[:, q, :, 0], -1.0, xrs[:, q, :], ALU.mult, ALU.mult).then_inc(s_xsc, 1)

            def affine(q):
                v.wait_ge(s_xh, q + 1)
                bA = bnA[:, :].rearrange("p (a c) -> p a c", a=1).to_broadcast([P, tiles[q], H])
                bB = bnB[:, :].rearrange("p (a c) -> p a c", a=1).to_broadcast([P, tiles[q], H])
                link(v.tensor_tensor(hq[q], hq[q], bA, ALU.mult))
                v.tensor_tensor(hq[q], hq[q], bB, ALU.add).then_inc(s_aff, 1)

            stats(0)
            v.wait_ge(s_if, 1)
            link(v.tensor_tensor(cmp_f, idx_f[:, 2, :, :], idx_f[:, 1, :, :], ALU.is_equal))
            v.tensor_scalar(capw[:, :, :], cmp_f, 0.5, 2 * BIG, ALU.subtract, ALU.mult).then_inc(s_capc, 1)
            stats(1)
            affine(0)
            v.wait_ge(s_iT, 1)
            for a, column in enumerate((srcT, dstT)):
                for b in range(2):
                    o = 1024 * a + 512 * b
                    v.tensor_copy(column[:, b * 4 * RB:(b + 1) * 4 * RB], MT[:, o:o + 4 * RB]).then_inc(s_iTc, 1)
            stats(2)
            affine(1)
            v.wait_ge(s_nbp, 1)
            link(v.tensor_copy(nbf[:, :], PM[:, 0:K]))
            v.tensor_copy(nbi[:, :], nbf[0:1, :])
            v.tensor_tensor(dl[:, :, :], dstT[:, :].rearrange("p (k j) -> p k j", j=T),
                            nbf[:, :].rearrange("p (k a) -> p k a", a=1).to_broadcast([P, K, T]),
                            ALU.subtract).then_inc(s_nb, 1)
            stats(3)
            affine(2)
            affine(3)
            v.wait_ge(s_nb, 1)
            v.wait_ge(s_tab0, 1)
            v.wait_ge(s_par, 16 * 7)
            v.wait_ge(s_hnp, 16 * (XQ + 1))
            v.memset(carry[:, SLOTS - 1, 0:1], -BIG)
            link(v.memset(Mf[:, 1, CE - 1:CE], -BIG))

            def gap_onehot(k, slot, par, early):
                v.wait_ge(s_mT, k + 1)
                if not early:
                    v.wait_ge(s_sum, k - 1)
                v.scalar_tensor_tensor(ex[:, par, :, :].rearrange("p j c -> p (j c)"),
                                       S[:, slot, :, :].rearrange("p j c -> p (j c)"), tcol[:, 0:1],
                                       MT[:, 0:CE], ALU.mult, ALU.subtract).then_inc(s_d, 1)
                for j in range(T):
                    v.tensor_scalar(OH[:, par, j, :], iota[:, :], dl[:, k, j:j + 1] if isinstance(k, int) else dl[:, bass.ds(k, 1), j], None, ALU.is_equal)

            def scans(k, slot, par):
                v.wait_ge(s_evac, (k + 1) * 8)
                v.tensor_tensor_scan(Mf[:, par, :], cap[:, par, 0:CE], zT[:, par, :],
                                     Mf[:, 1 - par, CE - 1:CE], ALU.min, ALU.max).then_inc(s_fwd, 1)
                v.tensor_tensor(carry[:, slot, 0:1], Mf[:, 1 - par, CE - 1:CE], cap[:, par, 0:1], ALU.min).then_inc(s_cm, 1)
                v.wait_ge(s_fwd, k + 1)
                v.tensor_tensor_scan(Mb[:, par, ::-1], cap[:, par, 1:CE + 1][:, ::-1], Mf[:, par, ::-1],
                                     -BIG, ALU.min, ALU.max).then_inc(s_scan, 1)
                v.wait_ge(s_scan, k + 1)
                v.wait_ge(s_cm, k + 1)
                v.tensor_tensor(carry[:, slot, 1:2], carry[:, slot, 0:1], Mb[:, par, 0:1], ALU.subtract).then_inc(s_gap, 1)

            def merge(k, slot):
                v.wait_ge(s_sum, k + 1)
                v.wait_ge(s_fac, k + 1)
                nb = v.value_load(nbi[0:1, k:k + 1] if isinstance(k, int) else nbi[0:1, bass.ds(k, 1)], min_val=0, max_val=N)
                dn = DN[:, 0:256].rearrange("p (a n) -> p a n", a=2)
                if not isinstance(k, int) or k > 0:
                    v.wait_ge(s_mrg, k)
                v.scalar_tensor_tensor(tab[:, :, bass.ds(nb, 1)], tab[:, :, bass.ds(nb, 1)], fac[:, slot:slot + 1],
                                       dn[:, :, 0:1], ALU.mult, ALU.add)
                v.tensor_copy(tab[:, :, bass.ds(nb + 1, P - 1)], dn[:, :, 1:P]).then_inc(s_mrg, 1)

            def weight(k, slot, par):
                v.wait_ge(s_exp, k + 1)
                v.tensor_tensor(S[:, slot, :, :], S[:, slot, :, :], ex[:, par, :, :], ALU.mult).then_inc(s_p, 1)

            def step(k, u):
                peeled = isinstance(k, int)
                if not peeled or k >= 1:
                    gap_onehot(k - 1, (u - 1) % SLOTS, (u - 1) % 2, peeled and k - 1 < 2)
                if not peeled or k < K:
                    scans(k, u, u % 2)
                if not peeled or k >= 2:
                    merge(k - 2, (u - 2) % SLOTS)
                if not peeled or k >= 1:
                    weight(k - 1, (u - 1) % SLOTS, (u - 1) % 2)
            for k in range(SLOTS):
                step(k, k)
            with v.Fori(1, K // SLOTS - 1) as i:
                for u in range(SLOTS):
                    step(i * SLOTS + u, u)
            for k in range(K - SLOTS, K + 1):
                step(k, k % SLOTS)
            merge(K - 1, (K - 1) % SLOTS)
            v.wait_ge(s_mrg, K)

            L = [0]

            def mlp(m):
                wb = window(m)
                c = count[0]
                n = [0]

                def link2(ins):
                    n[0] += 1
                    ins.then_inc(s_act, 1)
                    v.wait_ge(s_act, m * 9 + n[0])
                D = tab[:, 0, bass.ds(wb, P)]
                Nn = tab[:, 1, bass.ds(wb, P)]
                link2(v.tensor_scalar(oT[:, 0, :], D, 1e-16, None, ALU.add))
                link2(v.reciprocal(oT[:, 1, :], oT[:, 0, :]))
                link2(v.scalar_tensor_tensor(oT[:, 2, :], D, SMEPS, Nn, ALU.mult, ALU.add))
                link2(v.tensor_tensor(oT[:, 2, :], oT[:, 2, :], oT[:, 1, :], ALU.mult))
                v.wait_ge(s_xT, m + 1)
                v.tensor_tensor(oT[:, 3, :], oT[:, 2, :], PM[:, 0:P], ALU.add).then_inc(s_o, 1)
                v.wait_ge(s_y, m + 1)
                link2(v.bn_stats(st[:, :], PM[:, 0:H2]))
                v.sem_inc(s_turn_dve, 1)
                link2(v.bn_aggr(mv[:, 0:2], st[:, :]))
                v.tensor_scalar(mv[:, 2:3], mv[:, 1:2], LNEPS, None, ALU.add).then_inc(s_var, 1)
                v.wait_ge(s_sd, m + 1)
                link2(v.reciprocal(mv[:, 4:5], mv[:, 3:4]))
                link2(v.tensor_tensor(mv[:, 6:7], mv[:, 0:1], mv[:, 4:5], ALU.mult))
                link2(v.tensor_scalar(mv[:, 5:6], mv[:, 6:7], -1.0, None, ALU.mult))
                v.tensor_copy(mv[:, 7:8], mv[:, 5:6]).then_inc(s_nrm, 1)
                v.wait_ge(s_o2, m + 1)
                if not isinstance(m, int) or m > 0:
                    v.wait_ge(s_out, m * 16)
                v.tensor_tensor(res[:, :], xw[:, :], PM[:, 0:H], ALU.add).then_inc(s_res, 1)
            mlp(0)
            with v.Fori(1, WT - 1) as m:
                mlp(m)
            mlp(WT - 1)

        @block.tensor
        def _(pe):
            pe.wait_ge(s_const, 5)
            pe.wait_ge(s_if, 1)
            for a in range(2):
                for b in range(NB):
                    o = 1024 * a + 512 * (b // 4) + RB * (b % 4)
                    ins = pe.transpose(MT[:, o:o + RB], idx_f[:, a, b, :], ident[0:RB, 0:RB])
            ins.then_inc(s_iT, 1)
            pe.wait_ge(s_iTc, 4)
            pe.matmul(PM[:, 0:K], ones_row[0:1, :], dstT[0:1, 0:K * T:T], start=True, stop=True).then_inc(s_nbp, 1)
            pe.wait_ge(s_nb, 1)

            def transposes(k, slot, par, early):
                rounds = (k // SLOTS + 1) * 16 if isinstance(k, int) else (k - slot) * (16 // SLOTS) + 16
                pe.wait_ge(s_capr[slot], rounds)
                for u in range(8):
                    g = u // 2
                    if not (early and u < 2):
                        pe.wait_ge(s_evac, k * 8 + u - 1)
                    if u % 2 == 0:
                        n = min(512, CE + 1 - 512 * g)
                        pe.matmul(ping[0][:, 0:n], ones_row16[0:1, :], capr[0:1, slot, 512 * g:512 * g + n],
                                  start=True, stop=True).then_inc(s_unit, 1)
                    else:
                        if u == 1:
                            pe.wait_ge(s_relu, k + 1)
                        for j in range(4 * g, min(4 * g + 4, T)):
                            ins = pe.transpose(ping[1][:, (j - 4 * g) * P:(j - 4 * g + 1) * P], S[:, slot, j, :], ident[:, :])
                        ins.then_inc(s_unit, 1)

            def max_transposes(k, par, early):
                pe.wait_ge(s_scan, k + 1)
                if not early:
                    pe.wait_ge(s_d, k)
                for j in range(T):
                    ins = pe.transpose(MT[:, j * P:(j + 1) * P], Mb[:, par, j * P:(j + 1) * P], ident[:, :])
                ins.then_inc(s_mT, 1)

            def sums(k, slot, par, early):
                pe.wait_ge(s_p, k + 1)
                if not early:
                    pe.wait_ge(s_mrg, k)
                for j in range(T):
                    pe.matmul(DN[:, 0:P], ex[:, par, j, :], OH[:, par, j, :], start=(j == 0), stop=(j == T - 1),
                              skip_group_check=True)
                    ins = pe.matmul(DN[:, P:2 * P], S[:, slot, j, :], OH[:, par, j, :], start=False, stop=(j == T - 1),
                                    skip_group_check=True)
                ins.then_inc(s_sum, 1)

            def step(k, u):
                peeled = isinstance(k, int)
                if not peeled or k < K:
                    transposes(k, u, u % 2, peeled and k == 0)
                    max_transposes(k, u % 2, peeled and k == 0)
                if not peeled or k >= 1:
                    sums(k - 1, (u - 1) % SLOTS, (u - 1) % 2, peeled and k == 1)
            for k in range(SLOTS):
                step(k, k)
            with pe.Fori(1, K // SLOTS - 1) as i:
                for u in range(SLOTS):
                    step(i * SLOTS + u, u)
            for k in range(K - SLOTS, K + 1):
                step(k, k % SLOTS)

            def mlp(m):
                pe.wait_ge(s_xw, (m + 1) * 32)
                if not isinstance(m, int) or m > 0:
                    pe.wait_ge(s_res, m)
                pe.transpose(PM[:, 0:P], hw[:, :], ident[:, :]).then_inc(s_xT, 1)
                pe.wait_ge(s_o, m + 1)
                pe.matmul(PM[:, 0:H2], oT[:, 3, :], w1s[:, :], start=True, stop=False)
                pe.matmul(PM[:, 0:H2], ones_row[0:1, :], b1s[0:1, :], start=False, stop=True).then_inc(s_y, 1)
                pe.wait_ge(s_yn, m + 1)
                pe.transpose(PM[:, 256:384], yn[:, 0:H], ident[:, :])
                pe.transpose(PM[:, 384:512], yn[:, H:H2], ident[:, :]).then_inc(s_yT, 1)
                pe.wait_ge(s_h2, m + 1)
                pe.matmul(PM[:, 0:H], h2[:, 0, :], w2s[:, 0, :], start=True, stop=False)
                pe.matmul(PM[:, 0:H], h2[:, 1, :], w2s[:, 1, :], start=False, stop=False)
                pe.matmul(PM[:, 0:H], ones_row[0:1, :], b2s[0:1, :], start=False, stop=True).then_inc(s_o2, 1)
            mlp(0)
            with pe.Fori(1, WT - 1) as m:
                mlp(m)
            mlp(WT - 1)


_INS = ['x', 'src', 'dst', 'edge_attr_128', 'L0_gnn_bn_weight', 'L0_gnn_bn_bias', 'L0_gnn_bn_mean', 'L0_gnn_bn_var',
        'L0_gnn_t', 'L0_gnn_W1', 'L0_gnn_b1', 'L0_gnn_ln_weight', 'L0_gnn_ln_bias', 'L0_gnn_W2', 'L0_gnn_b2']


def kernel(**inputs):
    import numpy as np
    import concourse.bacc as bacc
    from concourse.bass_utils import run_bass_kernel_spmd

    nc = bacc.Bacc("TRN2", target_bir_lowering=False, num_devices=1)
    arrays, args = {}, []
    for name in _INS:
        a = np.ascontiguousarray(inputs[name])
        arrays[f"in_{name}"] = a
        args.append(nc.dram_tensor(f"in_{name}", a.shape, mybir.dt.from_np(a.dtype), kind="ExternalInput").ap())
    args.append(nc.dram_tensor("out_rows", (N, H), FP32, kind="ExternalOutput").ap())
    build(nc, *args)
    r = run_bass_kernel_spmd(nc, [arrays], core_ids=[0])
    return r.results[0]["out_rows"]
```

```python
import concourse.bass as bass
from concourse import mybir
from contextlib import ExitStack

FP32 = mybir.dt.float32
BF16 = mybir.dt.bfloat16
I32 = mybir.dt.int32
ALU = mybir.AluOpType
ACT = mybir.ActivationFunctionType
AX = mybir.AxisListType

P = 128
N = 6250
E = 106250
H = 128
H2 = 2 * H
T = 13
CE = T * P
K = -(-E // CE)
EP = K * CE
SLOTS = 6
CAPS = 3
GROUPS = -(-T // 4)
DEPTH = 5
LOOPS = (K - SLOTS) // SLOTS
NB = 8
RB = EP // P // NB
NW = N + P
NWIN = -(-N // P)
BIG = 1.5e38
SMEPS = 1e-7
BNEPS = 1e-5
LNEPS = 1e-5


def build(nc, x, src, dst, ea, bn_w, bn_b, bn_m, bn_v, t_in, W1, b1, ln_w, ln_b, W2, b2, out):
    hn_dram = nc.dram_tensor("hn_rows", (N, H), FP32).ap()
    xh_dram = nc.dram_tensor("xh_rows", (N, H), FP32).ap()
    cap_dram = nc.dram_tensor("cap_row", (EP + 1,), BF16).ap()

    ctx = ExitStack()
    with ctx:
        def sb(name, shape, dt=FP32):
            return ctx.enter_context(nc.sbuf_tensor(name, shape, dt))

        def sem(name):
            return ctx.enter_context(nc.semaphore(name))

        ident = sb("ident", [P, P])
        iota = sb("iota", [P, P])
        ones_row = sb("ones_row", [1, P])
        c15 = sb("c15", [P, 1])
        ones_col = sb("ones_col", [P, 1])
        bnp = sb("bnp", [P, 4, H])
        bnA = sb("bnA", [P, H])
        bnB = sb("bnB", [P, H])
        tcol = sb("tcol", [P, 1])
        w1s = sb("w1s", [P, H2])
        w2s = sb("w2s", [P, 2, H])
        b1s = sb("b1s", [1, H2])
        b2s = sb("b2s", [1, H])
        lncol = sb("lncol", [P, 2, 2])
        capw = sb("capw", [RB, NB, P], BF16)
        cap0w = sb("cap0w", [1, 1], BF16)
        srcT = sb("srcT", [P, K * T])
        dstT = sb("dstT", [P, K * T])
        dl = sb("dl", [P, K, T])
        nbf = sb("nbf", [P, K])
        nbi = sb("nbi", [1, K], I32)
        nbc = sb("nbc", [1, K], I32)
        unsorted = sb("unsorted", [RB, NB, P])
        far = sb("far", [P, K * T + K])
        bad = sb("bad", [P, 4])
        badi = sb("badi", [1, 1], I32)
        gidx = sb("gidx", [P, SLOTS, T], I32)
        S = sb("S", [P, SLOTS, T, H])
        cap = sb("cap", [P, CAPS, CE + 1], BF16)
        zT = sb("zT", [P, 2, CE])
        MM = sb("MM", [P, 4, CE])
        Mf, Mb = MM[:, 0:2, :], MM[:, 2:4, :]
        ex = sb("ex", [P, 2, T, H])
        OH = sb("OH", [P, 2, T, P])
        def early(t, a):
            return t[0:RB, :, :, :].rearrange("r a j c -> r (a j c)")[:, 0:a * NB * P]
        idx_i = early(ex, 3).bitcast(I32).rearrange("r (a b p) -> r a b p", a=3, b=NB)
        idx_f = early(OH, 3).rearrange("r (a b p) -> r a b p", a=3, b=NB)
        cmp_f = early(ex, 1).rearrange("r (b p) -> r b p", b=NB)
        carry = sb("carry", [P, SLOTS, 2])
        fac = sb("fac", [P, SLOTS])
        tab = sb("tab", [P, 2, NW])
        xw = sb("xw", [P, 2, H])
        hw = sb("hw", [P, 2, H])
        oT = sb("oT", [P, 4, P])
        st = sb("st", [P, 6])
        xst = sb("xst", [P, T, 6])
        xmv = sb("xmv", [P, 4, T, 2])
        xrs = sb("xrs", [P, 4, T])
        xnm = sb("xnm", [P, 4, T])
        mv = sb("mv", [P, 8])
        mvi = sb("mvi", [P, 2], I32)
        nr = sb("nr", [P, 4])
        sc = sb("sc", [P, 2, 2])
        ys = sb("ys", [P, 2, H2])
        yn = sb("yn", [P, H2])
        h2 = sb("h2", [P, 2, P])
        res = sb("res", [P, 2, H])
        tile_dst = sb("tile_dst", [1, P], I32)
        tile_src = gidx[:, 0, 0:1]
        tile_msg, tile_r, tile_z = S[:, 0, 0, :], ex[:, 0, 0, :], ex[:, 0, 1, :]
        top = MM[:, :, :].rearrange("p a b -> p (a b)")
        pair = sb("pair", [P, 8])

        def pb(name):
            return ctx.enter_context(nc.psum_tensor(name, [P, 512], FP32))
        ping = [pb("ping0"), pb("ping1")]
        MT = ctx.enter_context(nc.psum_tensor("MT", [P, 2048], FP32))
        DN = pb("DN")
        PM = pb("PM")

        s_turn_sp = sem("sync_waited")
        s_turn_gp = sem("gpsimd_waited")
        s_turn_dve = sem("vector_waited")
        s_idx = sem("idx_rows_loaded")
        s_bn = sem("bn_loaded")
        s_x = [sem(f"x_piece_loaded{q}") for q in range(4)]
        s_xvar = sem("x_variance_ready")
        s_xsd = sem("x_std_ready")
        s_xsc = sem("x_scale_ready")
        s_h = sem("h_piece_ready")
        s_xh = sem("x_plus_h_ready")
        s_xhp = [sem(f"x_plus_h_stored{q}") for q in range(4)]
        s_par = sem("mlp_params_loaded")
        s_den = sem("denominator_ready")
        s_num = sem("numerator_ready")
        s_rec = sem("reciprocal_ready")
        s_agg = sem("aggregate_ready")
        s_st = sem("ln_stats_ready")
        s_mv = sem("ln_moments_ready")
        s_half = sem("ln_exponent_halved")
        s_capw = sem("cap_row_stored")
        s_const = sem("constants_ready")
        s_dve = sem("dve_steps")
        s_act = sem("act_steps")
        s_std = sem("bn_std_ready")
        s_ab = sem("bn_affine_ready")
        s_abT = sem("bn_affine_transposed")
        s_abc = sem("bn_columns_ready")
        s_aff = sem("hn_affine_done")
        s_hn = sem("hn_piece_ready")
        s_hnp = sem("hn_stored")
        s_if = sem("idx_float_ready")
        s_capc = sem("cap_rows_ready")
        s_iT = sem("idx_transposed")
        s_iTc = sem("idx_transposes_copied")
        s_nbp = sem("window_bases_broadcast")
        s_nb = sem("window_bases_ready")
        s_ea = [sem(f"edge_attr_loaded{q}") for q in range(SLOTS)]
        s_tail = sem("edge_attr_tail_loaded")
        s_capr = [sem(f"cap_loaded{q}") for q in range(CAPS)]
        s_gi = sem("gather_idx_ready")
        s_g = [sem(f"gathered{q}") for q in range(SLOTS)]
        s_relu = sem("relu_done")
        s_unit = sem("psum_unit_ready")
        s_evac = sem("psum_unit_evacuated")
        s_fwd = sem("forward_max_done")
        s_scan = sem("scans_done")
        s_cm = sem("carry_min_done")
        s_gap = sem("carry_gap_ready")
        s_mT = sem("max_transposed")
        s_d = sem("logit_gap_ready")
        s_fac = sem("carry_factor_ready")
        s_exp = sem("exp_done")
        s_p = sem("weighted_msg_ready")
        s_sum = sem("sums_ready")
        s_mrg = sem("chunk_merged")
        s_tab0 = sem("tables_cleared")
        s_xw = [sem(f"window_loaded{q}") for q in range(2)]
        s_bad = sem("general_path_flag_ready")
        s_uns = sem("unsorted_counted")
        s_far = sem("far_counted")
        s_badm = sem("violations_summed")
        s_tl = sem("tile_loaded")
        s_tg = sem("tile_gathered")
        s_tt = sem("tile_transposed")
        s_tr = sem("tile_messages_ready")
        s_tz = sem("tile_logits_ready")
        s_e1 = sem("edge_maximum_ready")
        s_e2 = sem("edge_exponents_ready")
        s_e3 = sem("edge_exps_ready")
        s_e4 = sem("edge_product_ready")
        s_edge = sem("edges_merged")
        s_xT = sem("x_window_transposed")
        s_hT = sem("hn_window_ready")
        s_o = sem("mlp_input_ready")
        s_y = sem("hidden_ready")
        s_ys = sem("hidden_copied")
        s_rs = sem("ln_scale_ready")
        s_var = sem("ln_guess_ready")
        s_ve = sem("ln_var_shifted")
        s_nt = sem("newton_steps")
        s_yn = sem("hidden_normalised")
        s_yT = sem("hidden_transposed")
        s_h2 = sem("hidden_activated")
        s_o2 = sem("mlp_output_ready")
        s_res = sem("result_ready")
        s_out = sem("result_stored")

        XQ, XJ = 4, N // P // 4
        XT = N - XQ * XJ * P
        tiles = [XJ, XJ, XJ, XJ + 1]
        xq = [S[:, q, 0:tiles[q], :] for q in range(XQ)]
        hbuf = (Mf[:, 0, :], Mf[:, 1, :], Mb[:, 0, :], Mb[:, 1, :])
        hq = [hbuf[q][:, 0:tiles[q] * H].rearrange("p (j c) -> p j c", c=H) for q in range(XQ)]

        def piece(rows, q):
            return rows[0:XQ * XJ * P, :].rearrange("(p q j) c -> q p j c", p=P, q=XQ)[q]

        class Chunk:
            def __init__(self, i, u):
                self.i, self.u = i + u // SLOTS, u % SLOTS
                self.k = self.i * SLOTS + self.u
                self.slot, self.par = self.u, self.u % 2
                self.peeled = isinstance(i, int)

            def back(self, n):
                return Chunk(self.i, self.u - n)

            def exists(self):
                return not self.peeled or 0 <= self.k < K

            def rounds(self, m):
                return self.i * (SLOTS // m) + self.u // m + 1

        def turns(eng, body, loops=LOOPS):
            for u in range(SLOTS):
                body(Chunk(0, u))
            with eng.Fori(1, loops + 1) as i:
                for u in range(SLOTS):
                    body(Chunk(i, u))
            for k in range((loops + 1) * SLOTS, K + DEPTH):
                body(Chunk(k // SLOTS, k % SLOTS))

        def wait_count(eng, s, n):
            if not isinstance(n, int) or n > 0:
                eng.wait_ge(s, n)

        flat = "p a b -> p (a b)"
        tiles_flat = "p j c -> p (j c)"
        dn = DN[:, 0:2 * P].rearrange("p (a n) -> p a n", a=2)

        def of(t, k):
            return t[0:1, k:k + 1] if isinstance(k, int) else t[0:1, bass.ds(k, 1)]

        FULL_TILES = E // P

        def general_tiles(eng, body):
            with eng.Fori(0, FULL_TILES) as t:
                body(t, t * P, 0)
            if E % P:
                body(FULL_TILES, E - P, P - E % P)

        def general_edges(eng, t, skip, body):
            with eng.Fori(skip, P) as e:
                body(e, t * P + e + (1 - skip))

        def general_windows(eng, body):
            with eng.Fori(0, NWIN - 1) as m:
                body(m + K, m * P)
            body(NWIN - 1 + K, N - P)

        def general(eng, body):
            eng.wait_ge(s_bad, 1)
            flag = eng.value_load(badi[0:1, 0:1])
            with eng.If(flag > 0):
                eng.wait_ge(s_out, 16 * K)
                body()

        block = ctx.enter_context(nc.Block())

        @block.sync
        def _(sp):
            for q in range(XQ):
                sp.dma_start(xq[q][:, 0:XJ, :], piece(x, q)).then_inc(s_x[q], 16)
            sp.dma_start(xq[XQ - 1][0:XT, XJ, :], x[N - XT:N, :]).then_inc(s_x[XQ - 1], 16)
            sp.dma_start(xq[XQ - 1][XT:P, XJ, :], x[0:P - XT, :]).then_inc(s_x[XQ - 1], 16)
            for q, v in enumerate((bn_w, bn_b, bn_m, bn_v)):
                sp.dma_start(bnp[:, q, :], v.rearrange("(a n) -> a n", a=1).to_broadcast([P, H])).then_inc(s_bn, 16)
            FULL = (NB - 1) * RB * P
            last_rows = (E - FULL) // P
            sp.wait_ge(s_const, 1)
            for a, (arr, o) in enumerate(((src, 0), (dst, 0), (dst, 1))):
                sp.dma_start(idx_i[:, a, 0:NB - 1, :],
                             arr[o:o + FULL].rearrange("(b r p) -> r b p", b=NB - 1, r=RB)).then_inc(s_idx, 16)
                sp.dma_start(idx_i[0:last_rows, a, NB - 1, :],
                             arr[FULL + o:FULL + o + last_rows * P].rearrange("(r p) -> r p", p=P)).then_inc(s_idx, 16)
                rest = E - FULL - last_rows * P - o
                sp.dma_start(idx_i[last_rows:last_rows + 1, a, NB - 1, 0:rest],
                             arr[E - rest:E].rearrange("(a n) -> a n", a=1)).then_inc(s_idx, 16)
            with nc.allow_non_contiguous_dma(reason="small parameter columns"):
                sp.dma_start(tcol[:, :], t_in.rearrange("(a n) -> a n", a=1).to_broadcast([P, 1])).then_inc(s_par, 16)
                sp.dma_start(lncol[:, 0, :], ln_w.rearrange("(h c) -> c h", c=H)).then_inc(s_par, 16)
                sp.dma_start(lncol[:, 1, :], ln_b.rearrange("(h c) -> c h", c=H)).then_inc(s_par, 16)
            sp.dma_start(w1s[:, :], W1).then_inc(s_par, 16)
            sp.dma_start(w2s[:, :, :], W2.rearrange("(h p) n -> p h n", p=P)).then_inc(s_par, 16)
            sp.dma_start(b1s[:, :], b1.rearrange("(a n) -> a n", a=1)).then_inc(s_par, 16)
            sp.dma_start(b2s[:, :], b2.rearrange("(a n) -> a n", a=1)).then_inc(s_par, 16)
            sp.wait_ge(s_capc, 1)
            for b in range(NB):
                sp.dma_start(cap_dram[1 + b * RB * P:1 + (b + 1) * RB * P].rearrange("(r p) -> r p", p=P),
                             capw[:, b, :]).then_inc(s_capw, 16)
            sp.dma_start(cap_dram[0:1].rearrange("(a n) -> a n", a=1), cap0w[:, :]).then_inc(s_capw, 16)

            def load_edges(c):
                if c.peeled and c.k == K - 1:
                    base = c.k * CE
                    full = (E - base) // P
                    rest = E - base - full * P
                    sp.dma_start(S[:, c.slot, 0:full, :],
                                 ea[base:base + full * P, :].rearrange("(j p) c -> p j c", p=P)).then_inc(s_tail, 16)
                    sp.dma_start(S[0:rest, c.slot, full, :], ea[E - rest:E, :]).then_inc(s_tail, 16)
                    sp.dma_start(S[rest:P, c.slot, full, :], ea[0:P - rest, :]).then_inc(s_tail, 16)
                    for j in range(full + 1, T):
                        sp.dma_start(S[:, c.slot, j, :], ea[0:P, :]).then_inc(s_tail, 16)
                else:
                    sp.dma_start(S[:, c.slot, :, :],
                                 ea[bass.ds(c.k * CE, CE), :].rearrange("(j p) c -> p j c", p=P)).then_inc(s_ea[c.slot], 16)

            def load_cap(c):
                b = c.u % CAPS
                sp.dma_start(cap[:, b, :], cap_dram[bass.ds(c.k * CE, CE + 1)].rearrange("(a n) -> a n", a=1)
                             .to_broadcast([P, CE + 1])).then_inc(s_capr[b], 16)

            for q in range(XQ):
                sp.wait_ge(s_xh, q + 1)
                sp.dma_start(piece(xh_dram, q), xq[q][:, 0:XJ, :]).then_inc(s_xhp[q], 16)
                if q == XQ - 1:
                    sp.dma_start(xh_dram[N - XT:N, :], xq[q][0:XT, XJ, :]).then_inc(s_xhp[q], 16)
                sp.wait_ge(s_hn, q + 1)
                sp.dma_start(piece(hn_dram, q), hq[q][:, 0:XJ, :]).then_inc(s_hnp, 16)
                if q == XQ - 1:
                    sp.dma_start(hn_dram[N - XT:N, :], hq[q][0:XT, XJ, :]).then_inc(s_hnp, 16)
                sp.wait_ge(s_xhp[q], 16 if q < XQ - 1 else 32)
                load_edges(Chunk(0, q))
            for u in range(XQ, SLOTS):
                load_edges(Chunk(0, u))
            sp.wait_ge(s_capw, 16 * (NB + 1))
            load_cap(Chunk(0, 0))
            sp.wait_ge(s_hnp, 16 * (XQ + 1))
            sp.wait_ge(s_nb, 1)

            def wait(s, n):
                if not isinstance(n, int) or n > 0:
                    sp.wait_ge(s, n)
                    sp.sem_inc(s_turn_sp, 1)

            def turn(c):
                w = c.back(5)
                if w.exists():
                    store_window(w.k, w.par, sp.value_load(of(nbc, w.k), min_val=0, max_val=N - P))
                w = c.back(3)
                if w.exists():
                    wait(s_res, w.k - 1)
                    load_window(w.par, sp.value_load(of(nbc, w.k), min_val=0, max_val=N - P))
                n = c.back(-1)
                if n.exists():
                    wait(s_gap, n.k - CAPS + 1)
                    load_cap(n)
                n = c.back(2 - SLOTS)
                if n.exists() and not (n.peeled and n.k < SLOTS):
                    wait(s_sum, n.k - SLOTS + 1)
                    load_edges(n)

            def load_window(par, base):
                sp.dma_start(xw[:, par, :], xh_dram[bass.ds(base, P), :]).then_inc(s_xw[par], 16)
                sp.dma_start(hw[:, par, :], hn_dram[bass.ds(base, P), :]).then_inc(s_xw[par], 16)

            def store_window(w, par, base):
                wait(s_out, 16 * w)
                wait(s_res, w + 1)
                sp.dma_start(out[bass.ds(base, P), :], res[:, par, :]).then_inc(s_out, 16)

            turns(sp, turn, LOOPS - 1)
            sp.wait_ge(s_out, 16 * K)

            def general_sync():
                def load_tile(t, base, skip):
                    wait(s_edge, t * P + 1)
                    sp.dma_start(tile_msg, ea[bass.ds(base, P), :]).then_inc(s_tl, 16)
                    with nc.allow_non_contiguous_dma(reason="a column of indices"):
                        sp.dma_start(tile_src, src[bass.ds(base, P)].rearrange("(n a) -> n a", a=1)).then_inc(s_tl, 16)
                    sp.dma_start(tile_dst[:, :], dst[bass.ds(base, P)].rearrange("(a n) -> a n", a=1)).then_inc(s_tl, 16)
                general_tiles(sp, load_tile)
                sp.wait_ge(s_edge, E + 1)

                def window(w, base):
                    wait(s_res, w)
                    load_window(0, base)
                    store_window(w, 0, base)
                general_windows(sp, window)
                sp.wait_ge(s_out, 16 * (K + NWIN))
            general(sp, general_sync)

        @block.gpsimd
        def _(gp):
            gp.memset(idx_i[:, 0, NB - 1, :], 0)
            gp.memset(idx_i[:, 1:3, NB - 1, :], N).then_inc(s_const, 1)
            gp.memset(ident[:, :], 0.0).then_inc(s_const, 1)
            gp.wait_ge(s_const, 2)
            gp.affine_select(out=ident[:, :], in_=ident[:, :], compare_op=ALU.not_equal, fill=1.0, base=0,
                             pattern=[[-1, P]], channel_multiplier=1).then_inc(s_const, 1)
            gp.iota(iota[:, :], [[1, P]], base=0, channel_multiplier=0,
                    allow_small_or_imprecise_dtypes=True).then_inc(s_const, 1)
            gp.memset(ones_row[:, :], 1.0)
            gp.memset(cap0w[:, :], -BIG)
            gp.memset(ones_col[:, :], 1.0)
            gp.memset(bad[:, :], 0.0)
            gp.memset(c15[:, :], 1.5).then_inc(s_const, 1)
            gp.memset(tab[:, :, :], 0.0).then_inc(s_tab0, 1)
            for q in range(XQ):
                gp.wait_ge(s_h, q + 1)
                gp.tensor_tensor(xq[q], xq[q], hq[q], ALU.add).then_inc(s_xh, 1)
            gp.wait_ge(s_hnp, 16 * (XQ + 1))

            def turn(c):
                if not c.exists():
                    return
                gp.wait_ge(s_gi, c.k + 1)
                if c.peeled and c.k == K - 1:
                    gp.wait_ge(s_tail, 16 * (3 + T - 1 - (E - c.k * CE) // P))
                else:
                    gp.wait_ge(s_ea[c.slot], 16 * c.rounds(SLOTS))
                gp.sem_inc(s_turn_gp, 1)
                for j in range(T):
                    gp.indirect_dma_start(S[:, c.slot, j, :], None, hn_dram[:, :],
                                          bass.IndirectOffsetOnAxis(ap=gidx[:, c.slot, j:j + 1], axis=0),
                                          compute_op=ALU.add).then_inc(s_g[c.slot], 16)
            turns(gp, turn)

            def general_gpsimd():
                def gather_tile(t, base, skip):
                    gp.wait_ge(s_tl, t * 48 + 48)
                    gp.sem_inc(s_turn_gp, 1)
                    gp.indirect_dma_start(tile_msg, None, hn_dram[:, :], bass.IndirectOffsetOnAxis(ap=tile_src, axis=0),
                                          compute_op=ALU.add).then_inc(s_tg, 16)
                general_tiles(gp, gather_tile)
            general(gp, general_gpsimd)

        @block.scalar
        def _(act):
            act.wait_ge(s_std, 1)
            act.activation(bnp[:, 3, :], bnp[:, 3, :], ACT.Sqrt).then_inc(s_std, 1)

            def normalise(q):
                act.wait_ge(s_xvar, q + 1)
                act.activation(xrs[:, q, 0:tiles[q]], xmv[:, q, 0:tiles[q], 1], ACT.Sqrt).then_inc(s_xsd, 1)
                act.wait_ge(s_xsc, q + 1)
                for j in range(tiles[q]):
                    ins = act.activation(hq[q][:, j, :], xq[q][:, j, :], ACT.Relu,
                                         bias=xnm[:, q, j:j + 1], scale=xrs[:, q, j:j + 1])
                ins.then_inc(s_h, 1)

            def relu_hn(q):
                act.wait_ge(s_aff, q + 1)
                act.activation(hq[q], hq[q], ACT.Relu).then_inc(s_hn, 1)
            normalise(0)
            for q in range(1, XQ):
                normalise(q)
                relu_hn(q - 1)
            relu_hn(XQ - 1)
            act.wait_ge(s_iTc, 2)

            def indices(c):
                act.activation(gidx[:, c.slot, :], srcT[:, bass.ds(c.k * T, T)], ACT.Copy).then_inc(s_gi, 1)
            for u in range(SLOTS):
                indices(Chunk(0, u))
            act.wait_ge(s_par, 16 * 7)

            def relu(c):
                act.wait_ge(s_g[c.slot], 16 * T * c.rounds(SLOTS))
                act.activation(S[:, c.slot, :, :], S[:, c.slot, :, :], ACT.Relu).then_inc(s_relu, 1)
                if c.back(-SLOTS).exists():
                    indices(c.back(-SLOTS))

            def evacuate(c):
                wait_count(act, s_gap, c.k - 1)
                for g in range(GROUPS):
                    n = min(512, CE - 512 * g)
                    act.wait_ge(s_unit, c.k * GROUPS + g + 1)
                    act.activation(zT[:, c.par, 512 * g:512 * g + n], ping[g % 2][:, 0:n], ACT.Copy,
                                   scale=tcol[:, 0:1]).then_inc(s_evac, 1)

            def exponentials(c):
                act.wait_ge(s_gap, c.k + 1)
                act.activation(fac[:, c.slot:c.slot + 1], carry[:, c.slot, 1:2], ACT.Exp).then_inc(s_fac, 1)
                act.wait_ge(s_d, c.k + 1)
                act.activation(ex[:, c.par, :, :], ex[:, c.par, :, :], ACT.Exp).then_inc(s_exp, 1)

            NEWTON = 9

            def hidden_copy(w, par):
                act.wait_ge(s_y, w + 1)
                wait_count(act, s_yn, w - 1)
                act.activation(ys[:, par, :], PM[:, 0:H2], ACT.Copy).then_inc(s_ys, 1)

            def hidden_scale(w, par):
                n = [0]

                def nlink(ins):
                    n[0] += 1
                    ins.then_inc(s_nt, 1)
                    act.wait_ge(s_nt, w * NEWTON + n[0])
                act.wait_ge(s_var, w + 1)
                y, scale = mv[:, 3:4], sc[:, par, 0:1]
                for step in range(3):
                    nlink(act.activation(nr[:, 0:1], y, ACT.Square))
                    nlink(act.activation(nr[:, 1:2], nr[:, 0:1], ACT.Identity, bias=c15[:, 0:1], scale=mv[:, 5:6]))
                    to = nr[:, 2:3] if step < 2 else scale
                    nlink(act.activation(to, y, ACT.Copy, scale=nr[:, 1:2]))
                    y = to
                act.activation(sc[:, par, 1:2], y, ACT.Copy, scale=mv[:, 6:7]).then_inc(s_rs, 1)

            def hidden_normalise(w, par):
                act.wait_ge(s_rs, w + 1)
                wait_count(act, s_yT, w)
                act.activation(yn[:, :], ys[:, par, :], ACT.Identity, bias=sc[:, par, 1:2], scale=sc[:, par, 0:1]).then_inc(s_yn, 1)

            def hidden_activate(w):
                act.wait_ge(s_yT, w + 1)
                for h in range(2):
                    ins = act.activation(h2[:, h, :], PM[:, 256 + 128 * h:384 + 128 * h], ACT.Relu,
                                         bias=lncol[:, 1, h:h + 1], scale=lncol[:, 0, h:h + 1])
                ins.then_inc(s_h2, 1)

            def turn(c):
                w, m = c.back(4), c.back(3)
                if c.exists():
                    evacuate(c)
                if c.back(-1).exists():
                    relu(c.back(-1))
                if w.exists():
                    hidden_scale(w.k, w.par)
                if c.back(1).exists():
                    exponentials(c.back(1))
                if m.exists():
                    hidden_copy(m.k, m.par)
                if w.exists():
                    hidden_normalise(w.k, w.par)
                    hidden_activate(w.k)
            relu(Chunk(0, 0))
            turns(act, turn, LOOPS - 1)

            def general_scalar():
                def edge(e, n):
                    act.wait_ge(s_e2, n)
                    act.activation(pair[:, 3:5], pair[:, 1:3], ACT.Exp).then_inc(s_e3, 1)

                def activate_tile(t, base, skip):
                    act.wait_ge(s_tt, t + 1)
                    act.activation(tile_r, PM[:, 0:P], ACT.Relu).then_inc(s_tr, 1)
                    act.wait_ge(s_tr, t + 1)
                    act.activation(tile_z, tile_r, ACT.Copy, scale=tcol[:, 0:1]).then_inc(s_tz, 1)
                    general_edges(act, t, skip, edge)
                general_tiles(act, activate_tile)

                def window(w, base):
                    hidden_copy(w, 0)
                    hidden_scale(w, 0)
                    hidden_normalise(w, 0)
                    hidden_activate(w)
                general_windows(act, window)
            general(act, general_scalar)

        @block.vector
        def _(v):
            count = [0]

            def link(ins):
                count[0] += 1
                ins.then_inc(s_dve, 1)
                v.wait_ge(s_dve, count[0])

            v.wait_ge(s_bn, 64)
            v.tensor_scalar(bnp[:, 3, :], bnp[:, 3, :], BNEPS, None, ALU.add).then_inc(s_std, 1)

            def stats(q):
                v.wait_ge(s_x[q], 16 if q < XQ - 1 else 48)
                for j in range(tiles[q]):
                    ins = v.bn_stats(xst[:, j, :], xq[q][:, j, :])
                link(ins)
                for j in range(tiles[q]):
                    ins = v.bn_aggr(xmv[:, q, j, :], xst[:, j, :])
                link(ins)
                n = tiles[q]
                v.tensor_scalar(xmv[:, q, 0:n, 1], xmv[:, q, 0:n, 1], LNEPS, None, ALU.add).then_inc(s_xvar, 1)
                v.wait_ge(s_xsd, q + 1)
                link(v.reciprocal(xrs[:, q, 0:n], xrs[:, q, 0:n]))
                v.scalar_tensor_tensor(xnm[:, q, 0:n], xmv[:, q, 0:n, 0], -1.0, xrs[:, q, 0:n], ALU.mult, ALU.mult).then_inc(s_xsc, 1)

            def affine(q):
                v.wait_ge(s_xh, q + 1)
                bA = bnA[:, :].rearrange("p (a c) -> p a c", a=1).to_broadcast([P, tiles[q], H])
                bB = bnB[:, :].rearrange("p (a c) -> p a c", a=1).to_broadcast([P, tiles[q], H])
                link(v.tensor_tensor(hq[q], hq[q], bA, ALU.mult))
                v.tensor_tensor(hq[q], hq[q], bB, ALU.add).then_inc(s_aff, 1)

            stats(0)
            v.wait_ge(s_std, 2)
            link(v.reciprocal(bnp[:, 3, :], bnp[:, 3, :]))
            link(v.tensor_tensor(bnA[:, :], bnp[:, 3, :], bnp[:, 0, :], ALU.mult))
            link(v.tensor_tensor(bnB[:, :], bnp[:, 2, :], bnA[:, :], ALU.mult))
            link(v.tensor_tensor(bnB[:, :], bnp[:, 1, :], bnB[:, :], ALU.subtract))
            stats(1)
            v.wait_ge(s_idx, 16 * 9)
            v.tensor_copy(idx_f, idx_i).then_inc(s_if, 1)
            v.wait_ge(s_if, 1)
            affine(0)
            link(v.tensor_tensor(cmp_f, idx_f[:, 2, :, :], idx_f[:, 1, :, :], ALU.is_equal))
            v.tensor_scalar(capw[:, :, :], cmp_f, 0.5, 2 * BIG, ALU.subtract, ALU.mult).then_inc(s_capc, 1)
            link(v.tensor_tensor(unsorted[:, :, :], idx_f[:, 2, :, :], idx_f[:, 1, :, :], ALU.is_lt))
            v.tensor_reduce(bad[0:RB, 0:1], unsorted[:, :, :].rearrange("r b p -> r (b p)"), axis=AX.X, op=ALU.add)
            stats(2)
            affine(1)
            v.wait_ge(s_iT, 1)
            for a, column in enumerate((srcT, dstT)):
                for b in range(2):
                    o = 1024 * a + 512 * b
                    v.tensor_copy(column[:, b * 4 * RB:(b + 1) * 4 * RB], MT[:, o:o + 4 * RB]).then_inc(s_iTc, 1)
            stats(3)
            affine(2)
            affine(3)
            v.wait_ge(s_nbp, 1)
            link(v.tensor_copy(nbf[:, :], PM[:, 0:K]))
            v.tensor_copy(nbi[:, :], nbf[0:1, :])
            v.tensor_scalar(nbc[:, :], nbf[0:1, :], float(N - P), None, ALU.min)
            v.wait_ge(s_iTc, 4)
            v.tensor_tensor(dl[:, :, :], dstT[:, :].rearrange("p (k j) -> p k j", j=T),
                            nbf[:, :].rearrange("p (k a) -> p k a", a=1).to_broadcast([P, K, T]),
                            ALU.subtract).then_inc(s_nb, 1)
            v.wait_ge(s_nb, 1)
            v.tensor_copy(far[:, 0:K * T], dl[:, :, :].rearrange("p k j -> p (k j)"))
            v.tensor_scalar(far[:, K * T:K * T + 1], nbf[:, 0:1], float(P - 1), None, ALU.add)
            link(v.tensor_tensor(far[:, K * T + 1:], nbf[:, 1:K], nbf[:, 0:K - 1], ALU.subtract))
            link(v.tensor_scalar(far[:, :], far[:, :], P - 0.5, None, ALU.is_gt))
            v.tensor_reduce(bad[:, 1:2], far[:, :], axis=AX.X, op=ALU.add).then_inc(s_far, 1)
            v.wait_ge(s_badm, 1)
            link(v.tensor_reduce(bad[0:1, 3:4], PM[0:1, 0:4], axis=AX.X, op=ALU.add))
            v.tensor_copy(badi[:, :], bad[0:1, 3:4]).then_inc(s_bad, 1)
            v.wait_ge(s_par, 16 * 7)
            v.wait_ge(s_hnp, 16 * (XQ + 1))
            v.wait_ge(s_tab0, 1)
            link(v.memset(Mf[:, 1, CE - 1:CE], -BIG))

            def gap(c):
                v.wait_ge(s_mT, c.k + 1)
                wait_count(v, s_sum, c.k - 1)
                v.scalar_tensor_tensor(ex[:, c.par, :, :].rearrange(tiles_flat), S[:, c.slot, :, :].rearrange(tiles_flat),
                                       tcol[:, 0:1], MT[:, 0:CE], ALU.mult, ALU.subtract).then_inc(s_d, 1)

            def onehot(c):
                wait_count(v, s_sum, c.k - 1)
                d = dl[:, c.k, :] if c.peeled else dl[:, bass.ds(c.k, 1), :].rearrange("p a j -> p (a j)")
                v.tensor_tensor(OH[:, c.par, :, :], iota[:, :].rearrange("p (a n) -> p a n", a=1).to_broadcast([P, T, P]),
                                d.rearrange("p (j a) -> p j a", a=1).to_broadcast([P, T, P]), ALU.is_equal)

            def forward_scan(c):
                v.wait_ge(s_capr[c.u % CAPS], 16 * c.rounds(CAPS))
                v.wait_ge(s_evac, (c.k + 1) * GROUPS)
                caps = cap[:, c.u % CAPS, :]
                before = Mf[:, 1 - c.par, CE - 1:CE]
                v.tensor_tensor_scan(Mf[:, c.par, :], caps[:, 0:CE], zT[:, c.par, :],
                                     before, ALU.min, ALU.max).then_inc(s_fwd, 1)
                v.tensor_tensor(carry[:, c.slot, 0:1], before, caps[:, 0:1], ALU.min).then_inc(s_cm, 1)

            def backward_scan(c):
                caps = cap[:, c.u % CAPS, :]
                v.wait_ge(s_fwd, c.k + 1)
                v.tensor_tensor_scan(Mb[:, c.par, ::-1], caps[:, 1:CE + 1][:, ::-1], Mf[:, c.par, ::-1],
                                     -BIG, ALU.min, ALU.max).then_inc(s_scan, 1)

            def carry_gap(c):
                v.wait_ge(s_scan, c.k + 1)
                v.wait_ge(s_cm, c.k + 1)
                v.tensor_tensor(carry[:, c.slot, 1:2], carry[:, c.slot, 0:1], Mb[:, c.par, 0:1], ALU.subtract).then_inc(s_gap, 1)

            def weight(c):
                v.wait_ge(s_exp, c.k + 1)
                v.tensor_tensor(S[:, c.slot, :, :], S[:, c.slot, :, :], ex[:, c.par, :, :], ALU.mult).then_inc(s_p, 1)

            def merge(c):
                v.wait_ge(s_sum, c.k + 1)
                v.wait_ge(s_fac, c.k + 1)
                nb = v.value_load(of(nbi, c.k), min_val=0, max_val=N)
                wait_count(v, s_mrg, c.k)
                v.scalar_tensor_tensor(tab[:, :, bass.ds(nb, 1)], tab[:, :, bass.ds(nb, 1)], fac[:, c.slot:c.slot + 1],
                                       dn[:, :, 0:1], ALU.mult, ALU.add)
                v.tensor_copy(tab[:, :, bass.ds(nb + 1, P - 1)], dn[:, :, 1:P]).then_inc(s_mrg, 1)

            def wait_own(s, n):
                v.wait_ge(s, n)
                v.sem_inc(s_turn_dve, 1)

            def aggregate(w, base):
                D = tab[:, 0, bass.ds(base, P)]
                v.tensor_scalar(oT[:, 0, :], D, 1e-16, None, ALU.add).then_inc(s_den, 1)
                v.scalar_tensor_tensor(oT[:, 2, :], D, SMEPS, tab[:, 1, bass.ds(base, P)], ALU.mult, ALU.add).then_inc(s_num, 1)
                v.wait_ge(s_den, w + 1)
                v.reciprocal(oT[:, 1, :], oT[:, 0, :]).then_inc(s_rec, 1)
                v.wait_ge(s_num, w + 1)
                v.wait_ge(s_rec, w + 1)
                v.tensor_tensor(oT[:, 2, :], oT[:, 2, :], oT[:, 1, :], ALU.mult).then_inc(s_agg, 1)

            def mlp_input(w):
                v.wait_ge(s_agg, w + 1)
                v.wait_ge(s_xT, w + 1)
                v.tensor_tensor(oT[:, 3, :], oT[:, 2, :], PM[:, 0:P], ALU.add).then_inc(s_o, 1)

            def hidden_stats(w, par):
                v.wait_ge(s_ys, w + 1)
                v.bn_stats(st[:, :], ys[:, par, :]).then_inc(s_st, 1)

            def hidden_moments(w):
                wait_own(s_st, w + 1)
                wait_count(v, s_rs, w)
                v.sem_inc(s_turn_dve, 1)
                v.bn_aggr(mv[:, 0:2], st[:, :]).then_inc(s_mv, 1)

            def hidden_guess(w):
                v.wait_ge(s_mv, w + 1)
                v.tensor_scalar(mv[:, 2:3], mv[:, 1:2], LNEPS, None, ALU.add).then_inc(s_ve, 1)
                v.tensor_scalar(mv[:, 6:7], mv[:, 0:1], -1.0, None, ALU.mult)
                v.wait_ge(s_ve, w + 1)
                v.tensor_scalar(mvi[:, 0:1], mv[:, 2:3].bitcast(I32), 1, None, ALU.logical_shift_right).then_inc(s_half, 1)
                v.tensor_scalar(mv[:, 5:6], mv[:, 2:3], -0.5, None, ALU.mult)
                v.wait_ge(s_half, w + 1)
                v.tensor_scalar(mv[:, 3:4].bitcast(I32), mvi[:, 0:1], -1.0, float(0x5f3759df), ALU.mult, ALU.add).then_inc(s_var, 1)

            def finish(w, par):
                v.wait_ge(s_o2, w + 1)
                wait_count(v, s_out, 16 * (w - 1))
                v.tensor_tensor(res[:, par, :], xw[:, par, :], PM[:, 0:H], ALU.add).then_inc(s_res, 1)

            def turn(c):
                b, m, w, f = c.back(1), c.back(3), c.back(4), c.back(5)
                if w.exists():
                    hidden_stats(w.k, w.par)
                if b.exists():
                    forward_scan(b)
                if w.exists():
                    hidden_moments(w.k)
                if f.exists():
                    finish(f.k, f.par)
                if b.exists():
                    backward_scan(b)
                if w.exists():
                    hidden_guess(w.k)
                if b.exists():
                    carry_gap(b)
                    onehot(b)
                if m.exists():
                    wait_own(s_mrg, m.k + 1)
                    aggregate(m.k, v.value_load(of(nbc, m.k), min_val=0, max_val=N - P))
                if b.exists():
                    gap(b)
                if m.exists():
                    mlp_input(m.k)
                if c.back(2).exists():
                    merge(c.back(2))
                if b.exists():
                    weight(b)
            turns(v, turn)

            def general_vector():
                v.memset(tab[:, :, :], 0.0)
                v.memset(top[:, 0:N], -BIG).then_inc(s_edge, 1)
                best = pair[:, 0:1]

                def edge(e, n):
                    node = v.value_load(tile_dst[0:1, bass.ds(e, 1)], min_val=0, max_val=N - 1)
                    so_far = top[:, bass.ds(node, 1)]
                    v.wait_ge(s_edge, n)
                    v.sem_inc(s_turn_dve, 1)
                    v.tensor_tensor(best, so_far, tile_z[:, bass.ds(e, 1)], ALU.max).then_inc(s_e1, 1)
                    v.wait_ge(s_e1, n)
                    v.sem_inc(s_turn_dve, 1)
                    v.tensor_tensor(pair[:, 1:2], so_far, best, ALU.subtract)
                    v.tensor_tensor(pair[:, 2:3], tile_z[:, bass.ds(e, 1)], best, ALU.subtract).then_inc(s_e2, 1)
                    v.wait_ge(s_e3, n)
                    v.sem_inc(s_turn_dve, 1)
                    v.tensor_tensor(pair[:, 5:6], tile_r[:, bass.ds(e, 1)], pair[:, 4:5], ALU.mult).then_inc(s_e4, 1)
                    v.scalar_tensor_tensor(tab[:, 0, bass.ds(node, 1)], tab[:, 0, bass.ds(node, 1)], pair[:, 3:4],
                                           pair[:, 4:5], ALU.mult, ALU.add)
                    v.tensor_copy(so_far, best)
                    v.wait_ge(s_e4, n)
                    v.sem_inc(s_turn_dve, 1)
                    v.scalar_tensor_tensor(tab[:, 1, bass.ds(node, 1)], tab[:, 1, bass.ds(node, 1)], pair[:, 3:4],
                                           pair[:, 5:6], ALU.mult, ALU.add).then_inc(s_edge, 1)

                def merge_tile(t, base, skip):
                    v.wait_ge(s_tz, t + 1)
                    v.sem_inc(s_turn_dve, 1)
                    general_edges(v, t, skip, edge)
                general_tiles(v, merge_tile)
                v.wait_ge(s_edge, E + 1)

                def window(w, base):
                    aggregate(w, base)
                    mlp_input(w)
                    hidden_stats(w, 0)
                    hidden_moments(w)
                    hidden_guess(w)
                    finish(w, 0)
                general_windows(v, window)
            general(v, general_vector)

        @block.tensor
        def _(pe):
            pe.wait_ge(s_const, 5)
            pe.wait_ge(s_if, 1)
            for a in range(2):
                for b in range(NB):
                    o = 1024 * a + 512 * (b // 4) + RB * (b % 4)
                    ins = pe.transpose(MT[:, o:o + RB], idx_f[:, a, b, :], ident[0:RB, 0:RB])
            ins.then_inc(s_iT, 1)
            pe.wait_ge(s_iTc, 4)
            pe.matmul(PM[:, 0:K], ones_row[0:1, :], dstT[0:1, 0:K * T:T], start=True, stop=True).then_inc(s_nbp, 1)
            pe.wait_ge(s_far, 1)
            pe.matmul(PM[0:1, 0:4], ones_col[:, :], bad[:, 0:4], start=True, stop=True).then_inc(s_badm, 1)
            pe.wait_ge(s_bad, 1)

            def transposes(c):
                pe.wait_ge(s_relu, c.k + 1)
                for g in range(GROUPS):
                    wait_count(pe, s_evac, c.k * GROUPS + g - 1)
                    for j in range(4 * g, min(4 * g + 4, T)):
                        ins = pe.transpose(ping[g % 2][:, (j - 4 * g) * P:(j - 4 * g + 1) * P], S[:, c.slot, j, :], ident[:, :])
                    ins.then_inc(s_unit, 1)

            def max_transposes(c):
                pe.wait_ge(s_scan, c.k + 1)
                wait_count(pe, s_d, c.k)
                for j in range(T):
                    ins = pe.transpose(MT[:, j * P:(j + 1) * P], Mb[:, c.par, j * P:(j + 1) * P], ident[:, :])
                ins.then_inc(s_mT, 1)

            def sums(c, tiles):
                if tiles[0] == 0:
                    pe.wait_ge(s_p, c.k + 1)
                    wait_count(pe, s_mrg, c.k)
                for j in tiles:
                    pe.matmul(DN[:, 0:P], ex[:, c.par, j, :], OH[:, c.par, j, :], start=(j == 0), stop=(j == T - 1),
                              skip_group_check=True)
                    ins = pe.matmul(DN[:, P:2 * P], S[:, c.slot, j, :], OH[:, c.par, j, :], start=False, stop=(j == T - 1),
                                    skip_group_check=True)
                if tiles[-1] == T - 1:
                    ins.then_inc(s_sum, 1)

            def hn_transpose(w, par, loads):
                pe.wait_ge(s_xw[par], 32 * loads)
                wait_count(pe, s_res, w - 1)
                pe.transpose(PM[:, 0:P], hw[:, par, :], ident[:, :]).then_inc(s_xT, 1)

            def hidden(w):
                pe.wait_ge(s_o, w + 1)
                pe.matmul(PM[:, 0:H2], oT[:, 3, :], w1s[:, :], start=True, stop=False)
                pe.matmul(PM[:, 0:H2], ones_row[0:1, :], b1s[0:1, :], start=False, stop=True).then_inc(s_y, 1)

            def hidden_transpose(w):
                pe.wait_ge(s_yn, w + 1)
                pe.transpose(PM[:, 256:384], yn[:, 0:H], ident[:, :])
                pe.transpose(PM[:, 384:512], yn[:, H:H2], ident[:, :]).then_inc(s_yT, 1)

            def project(w):
                pe.wait_ge(s_h2, w + 1)
                pe.matmul(PM[:, 0:H], h2[:, 0, :], w2s[:, 0, :], start=True, stop=False)
                pe.matmul(PM[:, 0:H], h2[:, 1, :], w2s[:, 1, :], start=False, stop=False)
                pe.matmul(PM[:, 0:H], ones_row[0:1, :], b2s[0:1, :], start=False, stop=True).then_inc(s_o2, 1)

            A = 4

            def turn(c):
                w, m, n = c.back(4), c.back(3), c.back(2)
                if c.exists():
                    transposes(c)
                if n.exists():
                    sums(n, range(0, A))
                if c.back(1).exists():
                    max_transposes(c.back(1))
                if m.exists():
                    hn_transpose(m.k, m.par, m.rounds(2))
                if n.exists():
                    sums(n, range(A, T))
                if m.exists():
                    hidden(m.k)
                if w.exists():
                    hidden_transpose(w.k)
                    project(w.k)
            turns(pe, turn)

            def general_tensor():
                def transpose_tile(t, base, skip):
                    pe.wait_ge(s_tg, t * 16 + 16)
                    pe.transpose(PM[:, 0:P], tile_msg, ident[:, :]).then_inc(s_tt, 1)
                general_tiles(pe, transpose_tile)

                def window(w, base):
                    hn_transpose(w, 0, w - K // 2 + 1)
                    hidden(w)
                    hidden_transpose(w)
                    project(w)
                general_windows(pe, window)
            general(pe, general_tensor)


_INS = ['x', 'src', 'dst', 'edge_attr_128', 'L0_gnn_bn_weight', 'L0_gnn_bn_bias', 'L0_gnn_bn_mean', 'L0_gnn_bn_var',
        'L0_gnn_t', 'L0_gnn_W1', 'L0_gnn_b1', 'L0_gnn_ln_weight', 'L0_gnn_ln_bias', 'L0_gnn_W2', 'L0_gnn_b2']


def kernel(**inputs):
    import numpy as np
    import concourse.bacc as bacc
    from concourse.bass_utils import run_bass_kernel_spmd

    nc = bacc.Bacc("TRN2", target_bir_lowering=False, num_devices=1)
    arrays, args = {}, []
    for name in _INS:
        a = np.ascontiguousarray(inputs[name])
        arrays[f"in_{name}"] = a
        args.append(nc.dram_tensor(f"in_{name}", a.shape, mybir.dt.from_np(a.dtype), kind="ExternalInput").ap())
    args.append(nc.dram_tensor("out_rows", (N, H), FP32, kind="ExternalOutput").ap())
    build(nc, *args)
    r = run_bass_kernel_spmd(nc, [arrays], core_ids=[0])
    return r.results[0]["out_rows"]
```

```python
import concourse.bass as bass
from concourse import mybir
from contextlib import ExitStack

FP32 = mybir.dt.float32
BF16 = mybir.dt.bfloat16
I32 = mybir.dt.int32
ALU = mybir.AluOpType
ACT = mybir.ActivationFunctionType
AX = mybir.AxisListType

P = 128
N = 6250
E = 106250
H = 128
H2 = 2 * H
T = 15
CE = T * P
K = -(-E // CE)
EP = K * CE
LAST = -(-(E - (K - 1) * CE) // P)
SLOTS = 6
XW = 3
CAPS = 3
GROUPS = -(-T // 4)
DEPTH = 5
LOOPS = (K - SLOTS) // SLOTS
NB = 8
RB = EP // P // NB
NW = N + P
NWIN = -(-N // P)
BIG = 1.5e38
SMEPS = 1e-7
BNEPS = 1e-5
LNEPS = 1e-5


def build(nc, x, src, dst, ea, bn_w, bn_b, bn_m, bn_v, t_in, W1, b1, ln_w, ln_b, W2, b2, out):
    hn_dram = nc.dram_tensor("hn_rows", (N, H), FP32).ap()
    xh_dram = nc.dram_tensor("xh_rows", (N, H), FP32).ap()
    cap_dram = nc.dram_tensor("cap_row", (EP + 1,), BF16).ap()

    ctx = ExitStack()
    with ctx:
        def sb(name, shape, dt=FP32):
            return ctx.enter_context(nc.sbuf_tensor(name, shape, dt))

        def sem(name):
            return ctx.enter_context(nc.semaphore(name))

        ident = sb("ident", [P, P])
        iota = sb("iota", [P, P])
        ones_row = sb("ones_row", [1, P])
        c15 = sb("c15", [P, 1])
        ones_col = sb("ones_col", [P, 1])
        tcol = sb("tcol", [P, 1])
        w1s = sb("w1s", [P, H2])
        w2s = sb("w2s", [P, 2, H])
        b1s = sb("b1s", [1, H2])
        b2s = sb("b2s", [1, H])
        lncol = sb("lncol", [P, 2, 2])
        cap0w = sb("cap0w", [1, 1], BF16)
        srcT = sb("srcT", [P, K * T])
        dstT = sb("dstT", [P, K * T])
        dl = dstT[:, :].rearrange("p (k j) -> p k j", j=T)
        nbf = sb("nbf", [P, K])
        nbi = sb("nbi", [1, K], I32)
        nbc = sb("nbc", [1, K], I32)
        bad = sb("bad", [P, 4])
        badi = sb("badi", [1, 1], I32)
        gidx = sb("gidx", [P, SLOTS, T], I32)
        S = sb("S", [P, SLOTS, T, H])
        cap = sb("cap", [P, CAPS, CE + 1], BF16)
        zT = sb("zT", [P, 2, CE])
        MM = sb("MM", [P, 4, CE])
        Mf, Mb = MM[:, 0:2, :], MM[:, 2:4, :]
        ex = sb("ex", [P, 2, T, H])
        OH = sb("OH", [P, 2, T, P])
        def early(t, a):
            return t[0:RB, :, :, :].rearrange("r a j c -> r (a j c)")[:, 0:a * NB * P]
        idx_i = early(ex, 3).bitcast(I32).rearrange("r (a b p) -> r a b p", a=3, b=NB)
        idx_f = early(OH, 3).rearrange("r (a b p) -> r a b p", a=3, b=NB)
        cmp_f = early(ex, 1).rearrange("r (b p) -> r b p", b=NB)
        unsorted = zT[0:RB, 0, 0:NB * P].rearrange("r (b p) -> r b p", b=NB)
        far = OH[:, 0, :, :].rearrange("p j c -> p (j c)")[:, 0:K * T + K]
        capw = cap[0:RB, CAPS - 1, 0:NB * P].rearrange("r (b p) -> r b p", b=NB)
        carry = sb("carry", [P, SLOTS, 2])
        fac = sb("fac", [P, SLOTS])
        tab = sb("tab", [P, 2, NW])
        xw = sb("xw", [P, XW, H])
        hw = sb("hw", [P, 2, H])
        oT = sb("oT", [P, 4, P])
        bnp = oT
        st = sb("st", [P, 6])
        xst = sb("xst", [P, T, 6])
        xmv = sb("xmv", [P, 4, T, 2])
        xrs = sb("xrs", [P, 4, T])
        xnm = sb("xnm", [P, 4, T])
        mv = sb("mv", [P, 8])
        mvi = sb("mvi", [P, 2], I32)
        nr = sb("nr", [P, 4])
        sc = sb("sc", [P, 2, 2])
        ys = sb("ys", [P, 2, H2])
        yn = sb("yn", [P, H2])
        h2 = sb("h2", [P, 2, P])
        res = sb("res", [P, 2, H])
        bnA, bnB = res[:, 0, :], res[:, 1, :]
        tile_dst = sb("tile_dst", [1, P], I32)
        tile_src = gidx[:, 0, 0:1]
        tile_msg, tile_r, tile_z = S[:, 0, 0, :], ex[:, 0, 0, :], ex[:, 0, 1, :]
        top = MM[:, :, :].rearrange("p a b -> p (a b)")
        pair = sb("pair", [P, 8])

        def pb(name):
            return ctx.enter_context(nc.psum_tensor(name, [P, 512], FP32))
        ping = [pb("ping0"), pb("ping1")]
        MT = ctx.enter_context(nc.psum_tensor("MT", [P, 2048], FP32))
        DN = pb("DN")
        PM = pb("PM")

        s_turn_sp = sem("sync_waited")
        s_turn_gp = sem("gpsimd_waited")
        s_turn_dve = sem("vector_waited")
        s_idx = sem("idx_rows_loaded")
        s_bn = sem("bn_loaded")
        s_x = [sem(f"x_piece_loaded{q}") for q in range(4)]
        s_xvar = sem("x_variance_ready")
        s_xsd = sem("x_std_ready")
        s_xsc = sem("x_scale_ready")
        s_h = sem("h_piece_ready")
        s_xh = sem("x_plus_h_ready")
        s_xhp = [sem(f"x_plus_h_stored{q}") for q in range(4)]
        s_par = sem("mlp_params_loaded")
        s_den = sem("denominator_ready")
        s_num = sem("numerator_ready")
        s_rec = sem("reciprocal_ready")
        s_agg = sem("aggregate_ready")
        s_st = sem("ln_stats_ready")
        s_mv = sem("ln_moments_ready")
        s_half = sem("ln_exponent_halved")
        s_capw = sem("cap_row_stored")
        s_const = sem("constants_ready")
        s_dve = sem("dve_steps")
        s_std = sem("bn_std_ready")
        s_hA = sem("h_times_A_ready")
        s_aff0 = sem("hn_affine_done_first")
        s_aff = sem("hn_affine_done")
        s_hn = sem("hn_piece_ready")
        s_hnp = sem("hn_stored")
        s_if = sem("idx_float_ready")
        s_capc = sem("cap_rows_ready")
        s_srcT = sem("src_transposed")
        s_dstT = sem("dst_transposed")
        s_iTc = sem("dst_columns_ready")
        s_iTs = sem("src_columns_ready")
        s_nbp = sem("window_bases_broadcast")
        s_nb = sem("window_bases_ready")
        s_ea = [sem(f"edge_attr_loaded{q}") for q in range(SLOTS)]
        s_tail = sem("edge_attr_tail_loaded")
        s_capr = [sem(f"cap_loaded{q}") for q in range(CAPS)]
        s_gi = sem("gather_idx_ready")
        s_g = [sem(f"gathered{q}") for q in range(SLOTS)]
        s_relu = sem("relu_done")
        s_unit = sem("psum_unit_ready")
        s_evac = sem("psum_unit_evacuated")
        s_fwd = sem("forward_max_done")
        s_scan = sem("scans_done")
        s_cm = sem("carry_min_done")
        s_gap = sem("carry_gap_ready")
        s_mT = sem("max_transposed")
        s_d = sem("logit_gap_ready")
        s_fac = sem("carry_factor_ready")
        s_exp = sem("exp_done")
        s_p = sem("weighted_msg_ready")
        s_sum = sem("sums_ready")
        s_mrg = sem("chunk_merged")
        s_tab0 = sem("tables_cleared")
        s_xw = [sem(f"x_window_loaded{q}") for q in range(XW)]
        s_hw = [sem(f"hn_window_loaded{q}") for q in range(2)]
        s_bad = sem("general_path_flag_ready")
        s_far = sem("far_counted")
        s_badm = sem("violations_summed")
        s_tl = sem("tile_loaded")
        s_tg = sem("tile_gathered")
        s_tt = sem("tile_transposed")
        s_tr = sem("tile_messages_ready")
        s_tz = sem("tile_logits_ready")
        s_e1 = sem("edge_maximum_ready")
        s_e2 = sem("edge_exponents_ready")
        s_e3 = sem("edge_exps_ready")
        s_e4 = sem("edge_product_ready")
        s_edge = sem("edges_merged")
        s_xT = sem("x_window_transposed")
        s_o = sem("mlp_input_ready")
        s_y = sem("hidden_ready")
        s_ys = sem("hidden_copied")
        s_rs = sem("ln_scale_ready")
        s_var = sem("ln_guess_ready")
        s_ve = sem("ln_var_shifted")
        s_nt = sem("newton_steps")
        s_yn = sem("hidden_normalised")
        s_yT = sem("hidden_transposed")
        s_h2 = sem("hidden_activated")
        s_o2 = sem("mlp_output_ready")
        s_res = sem("result_ready")
        s_out = sem("result_stored")

        XQ, XJ = 4, N // P // 4
        XT = N - XQ * XJ * P
        tiles = [XJ, XJ, XJ, XJ + 1]
        XS = SLOTS - XQ
        xq = [S[:, XS + q, 0:tiles[q], :] for q in range(XQ)]
        hbuf = (Mf[:, 0, :], Mf[:, 1, :], Mb[:, 0, :], Mb[:, 1, :])
        hq = [hbuf[q][:, 0:tiles[q] * H].rearrange("p (j c) -> p j c", c=H) for q in range(XQ)]

        def bnB_rows(q):
            return bnB.rearrange("p (a c) -> p a c", a=1).to_broadcast([P, tiles[q], H])

        def piece(rows, q):
            return rows[0:XQ * XJ * P, :].rearrange("(p q j) c -> q p j c", p=P, q=XQ)[q]

        class Chunk:
            def __init__(self, i, u):
                self.i, self.u = i + u // SLOTS, u % SLOTS
                self.k = self.i * SLOTS + self.u
                self.slot, self.par = self.u, self.u % 2
                self.peeled = isinstance(i, int)
                self.last = self.peeled and self.k == K - 1
                self.tiles = LAST if self.last else T
                self.edges = self.tiles * P
                self.groups = -(-self.tiles // 4)
                half = (self.tiles + 1) // 2
                self.halves = ((0, half), (half, self.tiles))

            def back(self, n):
                return Chunk(self.i, self.u - n)

            def exists(self):
                return not self.peeled or 0 <= self.k < K

            def rounds(self, m):
                return self.i * (SLOTS // m) + self.u // m + 1

        def turns(eng, body, loops=LOOPS):
            for u in range(SLOTS):
                body(Chunk(0, u))
            with eng.Fori(1, loops + 1) as i:
                for u in range(SLOTS):
                    body(Chunk(i, u))
            for k in range((loops + 1) * SLOTS, K + DEPTH):
                body(Chunk(k // SLOTS, k % SLOTS))

        def wait_count(eng, s, n):
            if not isinstance(n, int) or n > 0:
                eng.wait_ge(s, n)

        tiles_flat = "p j c -> p (j c)"
        dn = DN[:, 0:2 * P].rearrange("p (a n) -> p a n", a=2)

        def of(t, k):
            return t[0:1, k:k + 1] if isinstance(k, int) else t[0:1, bass.ds(k, 1)]

        FULL_TILES = E // P

        def general_tiles(eng, body):
            with eng.Fori(0, FULL_TILES) as t:
                body(t, t * P, 0)
            if E % P:
                body(FULL_TILES, E - P, P - E % P)

        def general_edges(eng, t, skip, body):
            with eng.Fori(skip, P) as e:
                body(e, t * P + e + (1 - skip))

        def general_windows(eng, body):
            with eng.Fori(0, NWIN - 1) as m:
                body(m + K, m * P)
            body(NWIN - 1 + K, N - P)

        def general(eng, body):
            eng.wait_ge(s_bad, 1)
            flag = eng.value_load(badi[0:1, 0:1])
            with eng.If(flag > 0):
                eng.wait_ge(s_out, 16 * K)
                body()

        block = ctx.enter_context(nc.Block())

        @block.sync
        def _(sp):
            def load_x(q):
                sp.dma_start(xq[q][:, 0:XJ, :], piece(x, q)).then_inc(s_x[q], 16)

            load_x(0)
            FULL = (NB - 1) * RB * P
            last_rows = (E - FULL) // P
            sp.wait_ge(s_const, 1)
            for a, (arr, o) in enumerate(((src, 0), (dst, 0), (dst, 1))):
                sp.dma_start(idx_i[:, a, 0:NB - 1, :],
                             arr[o:o + FULL].rearrange("(b r p) -> r b p", b=NB - 1, r=RB)).then_inc(s_idx, 16)
                sp.dma_start(idx_i[0:last_rows, a, NB - 1, :],
                             arr[FULL + o:FULL + o + last_rows * P].rearrange("(r p) -> r p", p=P)).then_inc(s_idx, 16)
                rest = E - FULL - last_rows * P - o
                sp.dma_start(idx_i[last_rows:last_rows + 1, a, NB - 1, 0:rest],
                             arr[E - rest:E].rearrange("(a n) -> a n", a=1)).then_inc(s_idx, 16)
            load_x(1)
            for q, v in enumerate((bn_w, bn_b, bn_m, bn_v)):
                sp.dma_start(bnp[:, q, :], v.rearrange("(a n) -> a n", a=1).to_broadcast([P, H])).then_inc(s_bn, 16)
            load_x(2)
            load_x(3)
            sp.dma_start(xq[XQ - 1][0:XT, XJ, :], x[N - XT:N, :]).then_inc(s_x[XQ - 1], 16)
            sp.dma_start(xq[XQ - 1][XT:P, XJ, :], x[0:P - XT, :]).then_inc(s_x[XQ - 1], 16)
            with nc.allow_non_contiguous_dma(reason="small parameter columns"):
                sp.dma_start(tcol[:, :], t_in.rearrange("(a n) -> a n", a=1).to_broadcast([P, 1])).then_inc(s_par, 16)
                sp.dma_start(lncol[:, 0, :], ln_w.rearrange("(h c) -> c h", c=H)).then_inc(s_par, 16)
                sp.dma_start(lncol[:, 1, :], ln_b.rearrange("(h c) -> c h", c=H)).then_inc(s_par, 16)
            sp.dma_start(w1s[:, :], W1).then_inc(s_par, 16)
            sp.dma_start(w2s[:, :, :], W2.rearrange("(h p) n -> p h n", p=P)).then_inc(s_par, 16)
            sp.dma_start(b1s[:, :], b1.rearrange("(a n) -> a n", a=1)).then_inc(s_par, 16)
            sp.dma_start(b2s[:, :], b2.rearrange("(a n) -> a n", a=1)).then_inc(s_par, 16)
            def load_edges(c):
                if c.last:
                    base = c.k * CE
                    full = (E - base) // P
                    rest = E - base - full * P
                    sp.dma_start(S[:, c.slot, 0:full, :],
                                 ea[base:base + full * P, :].rearrange("(j p) c -> p j c", p=P)).then_inc(s_tail, 16)
                    sp.dma_start(S[0:rest, c.slot, full, :], ea[E - rest:E, :]).then_inc(s_tail, 16)
                    sp.dma_start(S[rest:P, c.slot, full, :], ea[0:P - rest, :]).then_inc(s_tail, 16)
                else:
                    sp.dma_start(S[:, c.slot, :, :],
                                 ea[bass.ds(c.k * CE, CE), :].rearrange("(j p) c -> p j c", p=P)).then_inc(s_ea[c.slot], 16)

            def load_cap(c):
                b = c.u % CAPS
                sp.dma_start(cap[:, b, :], cap_dram[bass.ds(c.k * CE, CE + 1)].rearrange("(a n) -> a n", a=1)
                             .to_broadcast([P, CE + 1])).then_inc(s_capr[b], 16)

            for u in range(XS):
                load_edges(Chunk(0, u))

            def store_xh(q):
                sp.wait_ge(s_xh, q + 1)
                sp.dma_start(piece(xh_dram, q), xq[q][:, 0:XJ, :]).then_inc(s_xhp[q], 16)

            def store_hn(q):
                sp.wait_ge(s_hn, q + 1)
                sp.dma_start(piece(hn_dram, q), hq[q][:, 0:XJ, :]).then_inc(s_hnp, 16)

            for q in range(XQ - 1):
                store_xh(q)
            for q in range(XQ - 1):
                store_hn(q)
            store_xh(XQ - 1)
            sp.dma_start(xh_dram[N - XT:N, :], xq[XQ - 1][0:XT, XJ, :]).then_inc(s_xhp[XQ - 1], 16)
            store_hn(XQ - 1)
            sp.dma_start(hn_dram[N - XT:N, :], hq[XQ - 1][0:XT, XJ, :]).then_inc(s_hnp, 16)
            sp.wait_ge(s_capc, 1)
            for b in range(NB):
                sp.dma_start(cap_dram[1 + b * RB * P:1 + (b + 1) * RB * P].rearrange("(r p) -> r p", p=P),
                             capw[:, b, :]).then_inc(s_capw, 16)
            sp.dma_start(cap_dram[0:1].rearrange("(a n) -> a n", a=1), cap0w[:, :]).then_inc(s_capw, 16)

            for q in range(XQ):
                sp.wait_ge(s_xhp[q], 16 if q < XQ - 1 else 32)
                load_edges(Chunk(0, XS + q))
            sp.wait_ge(s_capw, 16 * (NB + 1))
            load_cap(Chunk(0, 0))
            sp.wait_ge(s_hnp, 16 * (XQ + 1))
            sp.wait_ge(s_nb, 1)

            def wait(s, n):
                if not isinstance(n, int) or n > 0:
                    sp.wait_ge(s, n)
                    sp.sem_inc(s_turn_sp, 1)

            def turn(c):
                w = c.back(5)
                if w.exists():
                    store_window(w.k, w.par, sp.value_load(of(nbc, w.k), min_val=0, max_val=N - P))
                w = c.back(2)
                if w.exists():
                    wait(s_res, w.k - XW + 1)
                    wait(s_xT, w.k - 1)
                    load_window(w.u % XW, w.par, sp.value_load(of(nbc, w.k), min_val=0, max_val=N - P))
                n = c.back(-1)
                if n.exists():
                    wait(s_gap, n.k - CAPS + 1)
                    load_cap(n)
                n = c.back(2 - SLOTS)
                if n.exists() and not (n.peeled and n.k < SLOTS):
                    wait(s_sum, n.k - SLOTS + 1)
                    load_edges(n)

            def load_window(xb, hb, base):
                sp.dma_start(xw[:, xb, :], xh_dram[bass.ds(base, P), :]).then_inc(s_xw[xb], 16)
                sp.dma_start(hw[:, hb, :], hn_dram[bass.ds(base, P), :]).then_inc(s_hw[hb], 16)

            def store_window(w, par, base):
                wait(s_out, 16 * w)
                wait(s_res, w + 1)
                sp.dma_start(out[bass.ds(base, P), :], res[:, par, :]).then_inc(s_out, 16)

            turns(sp, turn, LOOPS - 1)
            sp.wait_ge(s_out, 16 * K)

            def general_sync():
                def load_tile(t, base, skip):
                    wait(s_edge, t * P + 1)
                    sp.dma_start(tile_msg, ea[bass.ds(base, P), :]).then_inc(s_tl, 16)
                    with nc.allow_non_contiguous_dma(reason="a column of indices"):
                        sp.dma_start(tile_src, src[bass.ds(base, P)].rearrange("(n a) -> n a", a=1)).then_inc(s_tl, 16)
                    sp.dma_start(tile_dst[:, :], dst[bass.ds(base, P)].rearrange("(a n) -> a n", a=1)).then_inc(s_tl, 16)
                general_tiles(sp, load_tile)
                sp.wait_ge(s_edge, E + 1)

                def window(w, base):
                    wait(s_res, w)
                    load_window(0, 0, base)
                    store_window(w, 0, base)
                general_windows(sp, window)
                sp.wait_ge(s_out, 16 * (K + NWIN))
            general(sp, general_sync)

        @block.gpsimd
        def _(gp):
            gp.memset(cap0w[:, :], -BIG)
            gp.memset(bad[:, :], 0.0)
            gp.memset(idx_i[:, 0, NB - 1, :], 0)
            gp.memset(idx_i[:, 1:3, NB - 1, :], N).then_inc(s_const, 1)
            gp.memset(ident[:, :], 0.0).then_inc(s_const, 1)
            gp.wait_ge(s_const, 2)
            gp.affine_select(out=ident[:, :], in_=ident[:, :], compare_op=ALU.not_equal, fill=1.0, base=0,
                             pattern=[[-1, P]], channel_multiplier=1).then_inc(s_const, 1)
            gp.iota(iota[:, :], [[1, P]], base=0, channel_multiplier=0,
                    allow_small_or_imprecise_dtypes=True).then_inc(s_const, 1)
            gp.memset(ones_row[:, :], 1.0)
            gp.memset(ones_col[:, :], 1.0)
            gp.memset(c15[:, :], 1.5).then_inc(s_const, 1)
            gp.memset(tab[:, :, :], 0.0).then_inc(s_tab0, 1)
            for q in range(XQ):
                if q == XQ - 1:
                    gp.wait_ge(s_hA, 1)
                    gp.tensor_tensor(hq[0], hq[0], bnB_rows(0), ALU.add).then_inc(s_aff0, 1)
                gp.wait_ge(s_h, q + 1)
                gp.tensor_tensor(xq[q], xq[q], hq[q], ALU.add).then_inc(s_xh, 1)
            gp.wait_ge(s_hnp, 16 * (XQ + 1))

            def turn(c):
                if not c.exists():
                    return
                gp.wait_ge(s_gi, c.k + 1)
                if c.last:
                    gp.wait_ge(s_tail, 16 * 3)
                else:
                    gp.wait_ge(s_ea[c.slot], 16 * c.rounds(SLOTS))
                gp.sem_inc(s_turn_gp, 1)
                for j in range(c.tiles):
                    gp.indirect_dma_start(S[:, c.slot, j, :], None, hn_dram[:, :],
                                          bass.IndirectOffsetOnAxis(ap=gidx[:, c.slot, j:j + 1], axis=0),
                                          compute_op=ALU.add).then_inc(s_g[c.slot], 16)
            turns(gp, turn)

            def general_gpsimd():
                def gather_tile(t, base, skip):
                    gp.wait_ge(s_tl, t * 48 + 48)
                    gp.sem_inc(s_turn_gp, 1)
                    gp.indirect_dma_start(tile_msg, None, hn_dram[:, :], bass.IndirectOffsetOnAxis(ap=tile_src, axis=0),
                                          compute_op=ALU.add).then_inc(s_tg, 16)
                general_tiles(gp, gather_tile)
            general(gp, general_gpsimd)

        @block.scalar
        def _(act):
            def normalise(q):
                act.wait_ge(s_xvar, q + 1)
                act.activation(xrs[:, q, 0:tiles[q]], xmv[:, q, 0:tiles[q], 1], ACT.Sqrt).then_inc(s_xsd, 1)
                act.wait_ge(s_xsc, q + 1)
                for j in range(tiles[q]):
                    ins = act.activation(hq[q][:, j, :], xq[q][:, j, :], ACT.Relu,
                                         bias=xnm[:, q, j:j + 1], scale=xrs[:, q, j:j + 1])
                ins.then_inc(s_h, 1)

            def relu_hn(q):
                if q == 0:
                    act.wait_ge(s_aff0, 1)
                else:
                    act.wait_ge(s_aff, q)
                act.activation(hq[q], hq[q], ACT.Relu).then_inc(s_hn, 1)
            normalise(0)
            normalise(1)
            act.wait_ge(s_std, 1)
            act.activation(bnp[:, 3, :], bnp[:, 3, :], ACT.Sqrt).then_inc(s_std, 1)
            act.wait_ge(s_srcT, 1)
            for b in range(2):
                act.activation(srcT[:, b * 4 * RB:(b + 1) * 4 * RB], MT[:, 512 * b:512 * b + 4 * RB], ACT.Copy).then_inc(s_iTs, 1)
            normalise(2)
            normalise(3)
            for q in range(XQ):
                relu_hn(q)
            act.wait_ge(s_iTs, 2)

            def indices(c):
                act.activation(gidx[:, c.slot, :], srcT[:, bass.ds(c.k * T, T)], ACT.Copy).then_inc(s_gi, 1)
            for u in range(SLOTS):
                indices(Chunk(0, u))
            act.wait_ge(s_par, 16 * 7)

            def relu(c):
                act.wait_ge(s_g[c.slot], 16 * (T * c.rounds(SLOTS) - (T - c.tiles)))
                act.activation(S[:, c.slot, 0:c.tiles, :], S[:, c.slot, 0:c.tiles, :], ACT.Relu).then_inc(s_relu, 1)
                if c.back(-SLOTS).exists():
                    indices(c.back(-SLOTS))

            def evacuate(c):
                wait_count(act, s_gap, c.k - 1)
                for g in range(c.groups):
                    n = min(512, c.edges - 512 * g)
                    act.wait_ge(s_unit, c.k * GROUPS + g + 1)
                    act.activation(zT[:, c.par, 512 * g:512 * g + n], ping[g % 2][:, 0:n], ACT.Copy,
                                   scale=tcol[:, 0:1]).then_inc(s_evac, 1)

            def exponentials(c):
                act.wait_ge(s_gap, c.k + 1)
                act.activation(fac[:, c.slot:c.slot + 1], carry[:, c.slot, 1:2], ACT.Exp).then_inc(s_fac, 1)
                for n, (a, b) in enumerate(c.halves):
                    act.wait_ge(s_d, c.k * 2 + n + 1)
                    act.activation(ex[:, c.par, a:b, :], ex[:, c.par, a:b, :], ACT.Exp).then_inc(s_exp, 1)

            NEWTON = 9

            def hidden_copy(w, par):
                act.wait_ge(s_y, w + 1)
                wait_count(act, s_yn, w - 1)
                act.activation(ys[:, par, :], PM[:, 0:H2], ACT.Copy).then_inc(s_ys, 1)

            def hidden_scale(w, par):
                n = [0]

                def nlink(ins):
                    n[0] += 1
                    ins.then_inc(s_nt, 1)
                    act.wait_ge(s_nt, w * NEWTON + n[0])
                act.wait_ge(s_var, w + 1)
                y, scale = mv[:, 3:4], sc[:, par, 0:1]
                for step in range(3):
                    nlink(act.activation(nr[:, 0:1], y, ACT.Square))
                    nlink(act.activation(nr[:, 1:2], nr[:, 0:1], ACT.Identity, bias=c15[:, 0:1], scale=mv[:, 5:6]))
                    to = nr[:, 2:3] if step < 2 else scale
                    nlink(act.activation(to, y, ACT.Copy, scale=nr[:, 1:2]))
                    y = to
                act.activation(sc[:, par, 1:2], y, ACT.Copy, scale=mv[:, 6:7]).then_inc(s_rs, 1)

            def hidden_normalise(w, par):
                act.wait_ge(s_rs, w + 1)
                wait_count(act, s_yT, w)
                act.activation(yn[:, :], ys[:, par, :], ACT.Identity, bias=sc[:, par, 1:2], scale=sc[:, par, 0:1]).then_inc(s_yn, 1)

            def hidden_activate(w):
                act.wait_ge(s_yT, w + 1)
                for h in range(2):
                    ins = act.activation(h2[:, h, :], PM[:, 256 + 128 * h:384 + 128 * h], ACT.Relu,
                                         bias=lncol[:, 1, h:h + 1], scale=lncol[:, 0, h:h + 1])
                ins.then_inc(s_h2, 1)

            def turn(c):
                w, m = c.back(4), c.back(3)
                if c.exists():
                    evacuate(c)
                if w.exists():
                    hidden_scale(w.k, w.par)
                if c.back(1).exists():
                    exponentials(c.back(1))
                if c.back(-1).exists():
                    relu(c.back(-1))
                if m.exists():
                    hidden_copy(m.k, m.par)
                if w.exists():
                    hidden_normalise(w.k, w.par)
                    hidden_activate(w.k)
            relu(Chunk(0, 0))
            turns(act, turn, LOOPS - 1)

            def general_scalar():
                def edge(e, n):
                    act.wait_ge(s_e2, n)
                    act.activation(pair[:, 3:5], pair[:, 1:3], ACT.Exp).then_inc(s_e3, 1)

                def activate_tile(t, base, skip):
                    act.wait_ge(s_tt, t + 1)
                    act.activation(tile_r, PM[:, 0:P], ACT.Relu).then_inc(s_tr, 1)
                    act.wait_ge(s_tr, t + 1)
                    act.activation(tile_z, tile_r, ACT.Copy, scale=tcol[:, 0:1]).then_inc(s_tz, 1)
                    general_edges(act, t, skip, edge)
                general_tiles(act, activate_tile)

                def window(w, base):
                    hidden_copy(w, 0)
                    hidden_scale(w, 0)
                    hidden_normalise(w, 0)
                    hidden_activate(w)
                general_windows(act, window)
            general(act, general_scalar)

        @block.vector
        def _(v):
            count = [0]

            def link(ins):
                count[0] += 1
                ins.then_inc(s_dve, 1)
                v.wait_ge(s_dve, count[0])

            def stats(q):
                v.wait_ge(s_x[q], 16 if q < XQ - 1 else 48)
                for j in range(tiles[q]):
                    ins = v.bn_stats(xst[:, j, :], xq[q][:, j, :])
                link(ins)
                for j in range(tiles[q]):
                    ins = v.bn_aggr(xmv[:, q, j, :], xst[:, j, :])
                link(ins)
                n = tiles[q]
                v.tensor_scalar(xmv[:, q, 0:n, 1], xmv[:, q, 0:n, 1], LNEPS, None, ALU.add).then_inc(s_xvar, 1)
                v.wait_ge(s_xsd, q + 1)
                link(v.reciprocal(xrs[:, q, 0:n], xrs[:, q, 0:n]))
                v.scalar_tensor_tensor(xnm[:, q, 0:n], xmv[:, q, 0:n, 0], -1.0, xrs[:, q, 0:n], ALU.mult, ALU.mult).then_inc(s_xsc, 1)

            def affine(q):
                v.wait_ge(s_xh, q + 1)
                bA = bnA.rearrange("p (a c) -> p a c", a=1).to_broadcast([P, tiles[q], H])
                bB = bnB_rows(q)
                v.tensor_tensor(hq[q], hq[q], bA, ALU.mult).then_inc(s_hA, 1)
                if q > 0:
                    v.wait_ge(s_hA, q + 1)
                    v.tensor_tensor(hq[q], hq[q], bB, ALU.add).then_inc(s_aff, 1)

            stats(0)
            v.wait_ge(s_idx, 16 * 9)
            v.tensor_copy(idx_f[:, 0, :, :], idx_i[:, 0, :, :]).then_inc(s_if, 1)
            stats(1)
            v.wait_ge(s_bn, 64)
            v.tensor_scalar(bnp[:, 3, :], bnp[:, 3, :], BNEPS, None, ALU.add).then_inc(s_std, 1)
            stats(2)
            stats(3)
            v.wait_ge(s_std, 2)
            link(v.reciprocal(bnp[:, 3, :], bnp[:, 3, :]))
            link(v.tensor_tensor(bnA, bnp[:, 3, :], bnp[:, 0, :], ALU.mult))
            link(v.tensor_tensor(bnB, bnp[:, 2, :], bnA, ALU.mult))
            link(v.tensor_tensor(bnB, bnp[:, 1, :], bnB, ALU.subtract))
            for q in range(XQ):
                affine(q)
            v.tensor_copy(idx_f[:, 1:3, :, :], idx_i[:, 1:3, :, :]).then_inc(s_if, 1)
            v.wait_ge(s_if, 2)
            link(v.tensor_tensor(cmp_f, idx_f[:, 2, :, :], idx_f[:, 1, :, :], ALU.is_equal))
            v.tensor_scalar(capw, cmp_f, 0.5, 2 * BIG, ALU.subtract, ALU.mult).then_inc(s_capc, 1)
            link(v.tensor_tensor(unsorted, idx_f[:, 2, :, :], idx_f[:, 1, :, :], ALU.is_lt))
            v.tensor_reduce(bad[0:RB, 0:1], unsorted.rearrange("r b p -> r (b p)"), axis=AX.X, op=ALU.add)
            v.wait_ge(s_dstT, 1)
            for b in range(2):
                v.tensor_copy(dstT[:, b * 4 * RB:(b + 1) * 4 * RB], MT[:, 1024 + 512 * b:1024 + 512 * b + 4 * RB]).then_inc(s_iTc, 1)
            v.wait_ge(s_nbp, 1)
            link(v.tensor_copy(nbf[:, :], PM[:, 0:K]))
            v.tensor_copy(nbi[:, :], nbf[0:1, :])
            v.tensor_scalar(nbc[:, :], nbf[0:1, :], float(N - P), None, ALU.min)
            v.wait_ge(s_iTc, 2)
            v.tensor_tensor(dl, dl,
                            nbf[:, :].rearrange("p (k a) -> p k a", a=1).to_broadcast([P, K, T]),
                            ALU.subtract).then_inc(s_nb, 1)
            v.wait_ge(s_nb, 1)
            v.tensor_copy(far[:, 0:K * T], dstT[:, :])
            v.tensor_scalar(far[:, K * T:K * T + 1], nbf[:, 0:1], float(P - 1), None, ALU.add)
            link(v.tensor_tensor(far[:, K * T + 1:], nbf[:, 1:K], nbf[:, 0:K - 1], ALU.subtract))
            link(v.tensor_scalar(far, far, P - 0.5, None, ALU.is_gt))
            v.tensor_reduce(bad[:, 1:2], far, axis=AX.X, op=ALU.add).then_inc(s_far, 1)
            v.wait_ge(s_badm, 1)
            link(v.tensor_reduce(bad[0:1, 3:4], PM[0:1, 0:4], axis=AX.X, op=ALU.add))
            v.tensor_copy(badi[:, :], bad[0:1, 3:4]).then_inc(s_bad, 1)
            v.wait_ge(s_par, 16 * 7)
            v.wait_ge(s_hnp, 16 * (XQ + 1))
            v.wait_ge(s_tab0, 1)
            link(v.memset(Mf[:, 1, CE - 1:CE], -BIG))

            def gap(c):
                v.wait_ge(s_mT, c.k + 1)
                wait_count(v, s_sum, c.k - 1)
                for a, b in c.halves:
                    v.scalar_tensor_tensor(ex[:, c.par, a:b, :].rearrange(tiles_flat), S[:, c.slot, a:b, :].rearrange(tiles_flat),
                                           tcol[:, 0:1], MT[:, a * P:b * P], ALU.mult, ALU.subtract).then_inc(s_d, 1)

            def onehot(c):
                wait_count(v, s_sum, c.k - 1)
                d = dl[:, c.k, :] if c.peeled else dl[:, bass.ds(c.k, 1), :].rearrange("p a j -> p (a j)")
                n = c.tiles
                v.tensor_tensor(OH[:, c.par, 0:n, :], iota[:, :].rearrange("p (a n) -> p a n", a=1).to_broadcast([P, n, P]),
                                d[:, 0:n].rearrange("p (j a) -> p j a", a=1).to_broadcast([P, n, P]), ALU.is_equal)

            def forward_scan(c):
                v.wait_ge(s_capr[c.u % CAPS], 16 * c.rounds(CAPS))
                v.wait_ge(s_evac, c.k * GROUPS + c.groups)
                caps = cap[:, c.u % CAPS, :]
                before = Mf[:, 1 - c.par, CE - 1:CE]
                n = c.edges
                v.tensor_tensor_scan(Mf[:, c.par, 0:n], caps[:, 0:n], zT[:, c.par, 0:n],
                                     before, ALU.min, ALU.max).then_inc(s_fwd, 1)
                v.tensor_tensor(carry[:, c.slot, 0:1], before, caps[:, 0:1], ALU.min).then_inc(s_cm, 1)

            def backward_scan(c):
                caps = cap[:, c.u % CAPS, :]
                v.wait_ge(s_fwd, c.k + 1)
                n = c.edges
                v.tensor_tensor_scan(Mb[:, c.par, 0:n][:, ::-1], caps[:, 1:n + 1][:, ::-1], Mf[:, c.par, 0:n][:, ::-1],
                                     -BIG, ALU.min, ALU.max).then_inc(s_scan, 1)

            def carry_gap(c):
                v.wait_ge(s_scan, c.k + 1)
                v.wait_ge(s_cm, c.k + 1)
                v.tensor_tensor(carry[:, c.slot, 1:2], carry[:, c.slot, 0:1], Mb[:, c.par, 0:1], ALU.subtract).then_inc(s_gap, 1)

            def weight(c):
                for n, (a, b) in enumerate(c.halves):
                    v.wait_ge(s_exp, c.k * 2 + n + 1)
                    v.tensor_tensor(S[:, c.slot, a:b, :], S[:, c.slot, a:b, :], ex[:, c.par, a:b, :], ALU.mult).then_inc(s_p, 1)

            def merge(c):
                v.wait_ge(s_sum, c.k + 1)
                v.wait_ge(s_fac, c.k + 1)
                nb = v.value_load(of(nbi, c.k), min_val=0, max_val=N)
                wait_count(v, s_mrg, c.k)
                v.scalar_tensor_tensor(tab[:, :, bass.ds(nb, 1)], tab[:, :, bass.ds(nb, 1)], fac[:, c.slot:c.slot + 1],
                                       dn[:, :, 0:1], ALU.mult, ALU.add)
                v.tensor_copy(tab[:, :, bass.ds(nb + 1, P - 1)], dn[:, :, 1:P]).then_inc(s_mrg, 1)

            def wait_own(s, n):
                v.wait_ge(s, n)
                v.sem_inc(s_turn_dve, 1)

            def aggregate(w, base):
                D = tab[:, 0, bass.ds(base, P)]
                v.tensor_scalar(oT[:, 0, :], D, 1e-16, None, ALU.add).then_inc(s_den, 1)
                v.scalar_tensor_tensor(oT[:, 2, :], D, SMEPS, tab[:, 1, bass.ds(base, P)], ALU.mult, ALU.add).then_inc(s_num, 1)
                v.wait_ge(s_den, w + 1)
                v.reciprocal(oT[:, 1, :], oT[:, 0, :]).then_inc(s_rec, 1)
                v.wait_ge(s_num, w + 1)
                v.wait_ge(s_rec, w + 1)
                v.tensor_tensor(oT[:, 2, :], oT[:, 2, :], oT[:, 1, :], ALU.mult).then_inc(s_agg, 1)

            def mlp_input(w):
                v.wait_ge(s_agg, w + 1)
                v.wait_ge(s_xT, w + 1)
                v.tensor_tensor(oT[:, 3, :], oT[:, 2, :], PM[:, 0:P], ALU.add).then_inc(s_o, 1)

            def hidden_stats(w, par):
                v.wait_ge(s_ys, w + 1)
                v.bn_stats(st[:, :], ys[:, par, :]).then_inc(s_st, 1)

            def hidden_moments(w):
                wait_own(s_st, w + 1)
                wait_count(v, s_rs, w)
                v.sem_inc(s_turn_dve, 1)
                v.bn_aggr(mv[:, 0:2], st[:, :]).then_inc(s_mv, 1)

            def hidden_guess(w):
                v.wait_ge(s_mv, w + 1)
                v.tensor_scalar(mv[:, 2:3], mv[:, 1:2], LNEPS, None, ALU.add).then_inc(s_ve, 1)
                v.tensor_scalar(mv[:, 6:7], mv[:, 0:1], -1.0, None, ALU.mult)
                v.wait_ge(s_ve, w + 1)
                v.tensor_scalar(mvi[:, 0:1], mv[:, 2:3].bitcast(I32), 1, None, ALU.logical_shift_right).then_inc(s_half, 1)
                v.tensor_scalar(mv[:, 5:6], mv[:, 2:3], -0.5, None, ALU.mult)
                v.wait_ge(s_half, w + 1)
                v.tensor_scalar(mv[:, 3:4].bitcast(I32), mvi[:, 0:1], -1.0, float(0x5f3759df), ALU.mult, ALU.add).then_inc(s_var, 1)

            def finish(w, par, xb):
                v.wait_ge(s_o2, w + 1)
                wait_count(v, s_out, 16 * (w - 1))
                v.tensor_tensor(res[:, par, :], xw[:, xb, :], PM[:, 0:H], ALU.add).then_inc(s_res, 1)

            def turn(c):
                b, m, w, f = c.back(1), c.back(3), c.back(4), c.back(5)
                if w.exists():
                    hidden_stats(w.k, w.par)
                if b.exists():
                    forward_scan(b)
                if w.exists():
                    hidden_moments(w.k)
                if f.exists():
                    finish(f.k, f.par, f.u % XW)
                if b.exists():
                    backward_scan(b)
                if w.exists():
                    hidden_guess(w.k)
                if b.exists():
                    carry_gap(b)
                    onehot(b)
                if m.exists():
                    wait_own(s_mrg, m.k + 1)
                    aggregate(m.k, v.value_load(of(nbc, m.k), min_val=0, max_val=N - P))
                if b.exists():
                    gap(b)
                if m.exists():
                    mlp_input(m.k)
                if b.exists():
                    weight(b)
                if c.back(2).exists():
                    merge(c.back(2))
            turns(v, turn)

            def general_vector():
                v.memset(tab[:, :, :], 0.0)
                v.memset(top[:, 0:N], -BIG).then_inc(s_edge, 1)
                best = pair[:, 0:1]

                def edge(e, n):
                    node = v.value_load(tile_dst[0:1, bass.ds(e, 1)], min_val=0, max_val=N - 1)
                    so_far = top[:, bass.ds(node, 1)]
                    v.wait_ge(s_edge, n)
                    v.sem_inc(s_turn_dve, 1)
                    v.tensor_tensor(best, so_far, tile_z[:, bass.ds(e, 1)], ALU.max).then_inc(s_e1, 1)
                    v.wait_ge(s_e1, n)
                    v.sem_inc(s_turn_dve, 1)
                    v.tensor_tensor(pair[:, 1:2], so_far, best, ALU.subtract)
                    v.tensor_tensor(pair[:, 2:3], tile_z[:, bass.ds(e, 1)], best, ALU.subtract).then_inc(s_e2, 1)
                    v.wait_ge(s_e3, n)
                    v.sem_inc(s_turn_dve, 1)
                    v.tensor_tensor(pair[:, 5:6], tile_r[:, bass.ds(e, 1)], pair[:, 4:5], ALU.mult).then_inc(s_e4, 1)
                    v.scalar_tensor_tensor(tab[:, 0, bass.ds(node, 1)], tab[:, 0, bass.ds(node, 1)], pair[:, 3:4],
                                           pair[:, 4:5], ALU.mult, ALU.add)
                    v.tensor_copy(so_far, best)
                    v.wait_ge(s_e4, n)
                    v.sem_inc(s_turn_dve, 1)
                    v.scalar_tensor_tensor(tab[:, 1, bass.ds(node, 1)], tab[:, 1, bass.ds(node, 1)], pair[:, 3:4],
                                           pair[:, 5:6], ALU.mult, ALU.add).then_inc(s_edge, 1)

                def merge_tile(t, base, skip):
                    v.wait_ge(s_tz, t + 1)
                    v.sem_inc(s_turn_dve, 1)
                    general_edges(v, t, skip, edge)
                general_tiles(v, merge_tile)
                v.wait_ge(s_edge, E + 1)

                def window(w, base):
                    aggregate(w, base)
                    mlp_input(w)
                    hidden_stats(w, 0)
                    hidden_moments(w)
                    hidden_guess(w)
                    finish(w, 0, 0)
                general_windows(v, window)
            general(v, general_vector)

        @block.tensor
        def _(pe):
            pe.wait_ge(s_const, 5)

            def index_columns(a, done):
                pe.wait_ge(s_if, a + 1)
                for b in range(NB):
                    o = 1024 * a + 512 * (b // 4) + RB * (b % 4)
                    ins = pe.transpose(MT[:, o:o + RB], idx_f[:, a, b, :], ident[0:RB, 0:RB])
                ins.then_inc(done, 1)
            index_columns(0, s_srcT)
            index_columns(1, s_dstT)
            pe.wait_ge(s_iTc, 2)
            pe.wait_ge(s_iTs, 2)
            pe.matmul(PM[:, 0:K], ones_row[0:1, :], dstT[0:1, 0:K * T:T], start=True, stop=True).then_inc(s_nbp, 1)
            pe.wait_ge(s_far, 1)
            pe.matmul(PM[0:1, 0:4], ones_col[:, :], bad[:, 0:4], start=True, stop=True).then_inc(s_badm, 1)
            pe.wait_ge(s_bad, 1)

            def transposes(c):
                pe.wait_ge(s_relu, c.k + 1)
                for g in range(c.groups):
                    wait_count(pe, s_evac, c.k * GROUPS + g - 1)
                    for j in range(4 * g, min(4 * g + 4, c.tiles)):
                        ins = pe.transpose(ping[g % 2][:, (j - 4 * g) * P:(j - 4 * g + 1) * P], S[:, c.slot, j, :], ident[:, :])
                    ins.then_inc(s_unit, 1)

            def max_transposes(c):
                pe.wait_ge(s_scan, c.k + 1)
                wait_count(pe, s_d, 2 * c.k)
                for j in range(c.tiles):
                    ins = pe.transpose(MT[:, j * P:(j + 1) * P], Mb[:, c.par, j * P:(j + 1) * P], ident[:, :])
                ins.then_inc(s_mT, 1)

            def sums(c, tiles):
                if tiles[0] == 0:
                    pe.wait_ge(s_p, 2 * c.k + 2)
                    wait_count(pe, s_mrg, c.k)
                for j in tiles:
                    pe.matmul(DN[:, 0:P], ex[:, c.par, j, :], OH[:, c.par, j, :], start=(j == 0), stop=(j == c.tiles - 1),
                              skip_group_check=True)
                    ins = pe.matmul(DN[:, P:2 * P], S[:, c.slot, j, :], OH[:, c.par, j, :], start=False, stop=(j == c.tiles - 1),
                                    skip_group_check=True)
                if tiles[-1] == c.tiles - 1:
                    ins.then_inc(s_sum, 1)

            def hn_transpose(w, xb, xloads, par, loads):
                pe.wait_ge(s_xw[xb], 16 * xloads)
                pe.wait_ge(s_hw[par], 16 * loads)
                wait_count(pe, s_res, w - 1)
                pe.transpose(PM[:, 0:P], hw[:, par, :], ident[:, :]).then_inc(s_xT, 1)

            def hidden(w):
                pe.wait_ge(s_o, w + 1)
                pe.matmul(PM[:, 0:H2], oT[:, 3, :], w1s[:, :], start=True, stop=False)
                pe.matmul(PM[:, 0:H2], ones_row[0:1, :], b1s[0:1, :], start=False, stop=True).then_inc(s_y, 1)

            def hidden_transpose(w):
                pe.wait_ge(s_yn, w + 1)
                pe.transpose(PM[:, 256:384], yn[:, 0:H], ident[:, :])
                pe.transpose(PM[:, 384:512], yn[:, H:H2], ident[:, :]).then_inc(s_yT, 1)

            def project(w):
                pe.wait_ge(s_h2, w + 1)
                pe.matmul(PM[:, 0:H], h2[:, 0, :], w2s[:, 0, :], start=True, stop=False)
                pe.matmul(PM[:, 0:H], h2[:, 1, :], w2s[:, 1, :], start=False, stop=False)
                pe.matmul(PM[:, 0:H], ones_row[0:1, :], b2s[0:1, :], start=False, stop=True).then_inc(s_o2, 1)

            A = 4

            def turn(c):
                w, m, n = c.back(4), c.back(3), c.back(2)
                if c.exists():
                    transposes(c)
                if n.exists():
                    sums(n, range(0, A))
                if c.back(1).exists():
                    max_transposes(c.back(1))
                if m.exists():
                    hn_transpose(m.k, m.u % XW, m.rounds(XW), m.par, m.rounds(2))
                if n.exists():
                    sums(n, range(A, n.tiles))
                if m.exists():
                    hidden(m.k)
                if w.exists():
                    hidden_transpose(w.k)
                    project(w.k)
            turns(pe, turn)

            def general_tensor():
                def transpose_tile(t, base, skip):
                    pe.wait_ge(s_tg, t * 16 + 16)
                    pe.transpose(PM[:, 0:P], tile_msg, ident[:, :]).then_inc(s_tt, 1)
                general_tiles(pe, transpose_tile)

                def window(w, base):
                    hn_transpose(w, 0, w - K + -(-K // XW) + 1, 0, w - K + -(-K // 2) + 1)
                    hidden(w)
                    hidden_transpose(w)
                    project(w)
                general_windows(pe, window)
            general(pe, general_tensor)


_INS = ['x', 'src', 'dst', 'edge_attr_128', 'L0_gnn_bn_weight', 'L0_gnn_bn_bias', 'L0_gnn_bn_mean', 'L0_gnn_bn_var',
        'L0_gnn_t', 'L0_gnn_W1', 'L0_gnn_b1', 'L0_gnn_ln_weight', 'L0_gnn_ln_bias', 'L0_gnn_W2', 'L0_gnn_b2']


def kernel(**inputs):
    import numpy as np
    import concourse.bacc as bacc
    from concourse.bass_utils import run_bass_kernel_spmd

    nc = bacc.Bacc("TRN2", target_bir_lowering=False, num_devices=1)
    arrays, args = {}, []
    for name in _INS:
        a = np.ascontiguousarray(inputs[name])
        arrays[f"in_{name}"] = a
        args.append(nc.dram_tensor(f"in_{name}", a.shape, mybir.dt.from_np(a.dtype), kind="ExternalInput").ap())
    args.append(nc.dram_tensor("out_rows", (N, H), FP32, kind="ExternalOutput").ap())
    build(nc, *args)
    r = run_bass_kernel_spmd(nc, [arrays], core_ids=[0])
    return r.results[0]["out_rows"]
```
